# Optimizing a Trainium2 kernel written in Bass

```python
import numpy as np
import jax
import jax.numpy as jnp

def _softmax(x, axis=-1):
    return jax.nn.softmax(x, axis=axis)

def _gelu(x):
    return jax.nn.gelu(x, approximate=True)

def _silu(x):
    return jax.nn.silu(x)

def _sigmoid(x):
    return jax.nn.sigmoid(x)

def _layernorm(x, axis=-1, eps=1e-05):
    m = jnp.mean(x, axis=axis, keepdims=True)
    v = jnp.var(x, axis=axis, keepdims=True)
    return (x - m) / jnp.sqrt(v + eps)

def _scatter_add(tgt, idx, src, axis=0):
    return tgt.at[idx].add(src)

def _segment_sum(src, seg, n):
    return jax.ops.segment_sum(src, seg, n)
kernel_name = 'mk_seq_preln_d1_jaxref_r4_cd75f1'

def setup_inputs(seed: int=0):
    np.random.seed(seed)
    _w = jnp.asarray

    def _L0_attn_setup():
        import jax, jax.numpy as jnp
        import numpy as np
        B, N, H = (1, 1024, 512)
        NH, HD = (16, H // 16)
        WINDOW = 1024
        EPS = 1e-06
        THETA = 10000.0
        NEG = -1e+30

        def rmsnorm(x, w):
            var = jnp.mean(jnp.square(x.astype(jnp.float32)), axis=-1, keepdims=True)
            return (x * jax.lax.rsqrt(var + EPS)).astype(w.dtype) * w

        def rotate_half(x):
            x1, x2 = (x[..., :x.shape[-1] // 2], x[..., x.shape[-1] // 2:])
            return jnp.concatenate((-x2, x1), axis=-1)
        key = jax.random.key(seed)
        k1, k2, k3 = jax.random.split(key, 3)
        x = jax.random.normal(k1, (B, N, H), dtype=jnp.float32)
        w_qkv = jax.random.normal(k2, (H, 3 * H), dtype=jnp.float32) * (1.0 / np.sqrt(H))
        w_out = jax.random.normal(k3, (H, H), dtype=jnp.float32) * (1.0 / np.sqrt(H))
        q_gamma = jnp.ones((HD,), dtype=jnp.float32)
        k_gamma = jnp.ones((HD,), dtype=jnp.float32)
        return {'x': x, 'w_qkv': w_qkv, 'w_out': w_out, 'q_gamma': q_gamma, 'k_gamma': k_gamma}
    _L0_attn_in = _L0_attn_setup()

    def _L0_ffn_setup():
        import jax, jax.numpy as jnp
        import numpy as np
        BLOCK = 128
        MAXVAL = 448.0

        def _quant_dequant(x_flat):
            xb = x_flat.reshape(-1, BLOCK)
            s = jnp.max(jnp.abs(xb), axis=1, keepdims=True) / MAXVAL
            q = (xb / s).astype(jnp.float8_e4m3fn)
            return (q.astype(jnp.float32) * s).reshape(x_flat.shape)
        key = jax.random.key(seed)
        k1, k2 = jax.random.split(key)
        B, T, D, OUT = (4, 1024, 512, 512)
        x = jax.random.normal(k1, (B, T, D), dtype=jnp.float32)
        limit = float(np.sqrt(6.0 / (D + OUT)))
        weight = jax.random.uniform(k2, (OUT, D), minval=-limit, maxval=limit, dtype=jnp.float32)
        return {'x': x, 'weight': weight}
    _L0_ffn_in = _L0_ffn_setup()
    _d = {'L0_attn_x': _L0_attn_in['x'], 'L0_attn_w_qkv': _L0_attn_in['w_qkv'], 'L0_attn_w_out': _L0_attn_in['w_out'], 'L0_attn_q_gamma': _L0_attn_in['q_gamma'], 'L0_attn_k_gamma': _L0_attn_in['k_gamma'], 'L0_ffn_weight': _L0_ffn_in['weight']}
    _x0 = _d['L0_attn_x']
    _d['L0_attn_x'] = jax.random.normal(jax.random.fold_in(jax.random.key(seed), 1), (4, 512, 512), dtype=_x0.dtype)
    del _x0
    return _d

def reference(L0_attn_x, L0_attn_w_qkv, L0_attn_w_out, L0_attn_q_gamma, L0_attn_k_gamma, L0_ffn_weight):

    def _L0_attn_ref(x, w_qkv, w_out, q_gamma, k_gamma):
        import jax, jax.numpy as jnp
        import numpy as np
        B, N, H = (1, 1024, 512)
        NH, HD = (16, H // 16)
        WINDOW = 1024
        EPS = 1e-06
        THETA = 10000.0
        NEG = -1e+30

        def rmsnorm(x, w):
            var = jnp.mean(jnp.square(x.astype(jnp.float32)), axis=-1, keepdims=True)
            return (x * jax.lax.rsqrt(var + EPS)).astype(w.dtype) * w

        def rotate_half(x):
            x1, x2 = (x[..., :x.shape[-1] // 2], x[..., x.shape[-1] // 2:])
            return jnp.concatenate((-x2, x1), axis=-1)
        b, n, _ = x.shape
        qkv = jnp.einsum('bnh,hm->bnm', x, w_qkv)
        q, k, v = jnp.split(qkv, 3, axis=-1)
        q = q.reshape(b, n, NH, HD).transpose(0, 2, 1, 3)
        k = k.reshape(b, n, NH, HD).transpose(0, 2, 1, 3)
        v = v.reshape(b, n, NH, HD).transpose(0, 2, 1, 3)
        q = rmsnorm(q, q_gamma)
        k = rmsnorm(k, k_gamma)
        inv_freq = 1.0 / THETA ** (jnp.arange(0, HD, 2, dtype=jnp.float32) / HD)
        t = jnp.arange(n, dtype=jnp.float32)
        freqs = t[:, None] * inv_freq[None, :]
        emb = jnp.concatenate((freqs, freqs), axis=-1)
        cos = jnp.cos(emb)[None, None, :, :]
        sin = jnp.sin(emb)[None, None, :, :]
        q = q * cos + rotate_half(q) * sin
        k = k * cos + rotate_half(k) * sin
        kv_len = k.shape[-2]
        q_idx = jnp.arange(n)[:, None] + (kv_len - n)
        k_idx = jnp.arange(kv_len)[None, :]
        mask = (q_idx >= k_idx) & (q_idx - k_idx <= WINDOW)
        scores = jnp.einsum('bhqd,bhkd->bhqk', q, k) / np.sqrt(HD)
        scores = jnp.where(mask[None, None, :, :], scores, NEG)
        attn = jax.nn.softmax(scores, axis=-1)
        out = jnp.einsum('bhqk,bhkd->bhqd', attn, v)
        out = out.transpose(0, 2, 1, 3).reshape(b, n, H)
        return jnp.einsum('bnh,hm->bnm', out, w_out)

    def _L0_ffn_ref(x, weight):
        import jax, jax.numpy as jnp
        import numpy as np
        BLOCK = 128
        MAXVAL = 448.0

        def _quant_dequant(x_flat):
            xb = x_flat.reshape(-1, BLOCK)
            s = jnp.max(jnp.abs(xb), axis=1, keepdims=True) / MAXVAL
            q = (xb / s).astype(jnp.float8_e4m3fn)
            return (q.astype(jnp.float32) * s).reshape(x_flat.shape)
        B, T, D = x.shape
        x_deq = _quant_dequant(x.reshape(-1)).reshape(B * T, D)
        w_deq = _quant_dequant(weight.reshape(-1)).reshape(weight.shape)
        out = x_deq @ w_deq.T
        return out.reshape(B, T, -1)
    x = L0_attn_x
    x = x + _L0_attn_ref(_layernorm(x, axis=-1), L0_attn_w_qkv, L0_attn_w_out, L0_attn_q_gamma, L0_attn_k_gamma)
    x = x + _L0_ffn_ref(_layernorm(x, axis=-1), L0_ffn_weight)
    return x

_drawn_inputs = setup_inputs


def setup_inputs(seed=0):
    import zlib

    import numpy as np

    out = dict(_drawn_inputs(seed))
    spreads = {'L0_attn_q_gamma': (1.0, 0.2), 'L0_attn_k_gamma': (1.0, 0.551)}
    factors = {}
    for name, (base, spread) in spreads.items():
        noise = np.random.default_rng([zlib.crc32(name.encode()), seed]).standard_normal(out[name].shape)
        drawn = base * np.exp(spread * noise) if base else spread * noise
        out[name] = jnp.asarray(drawn.astype(out[name].dtype))
    for name, factor in factors.items():
        out[name] = (out[name] * factor).astype(out[name].dtype)
    return out
```

```python
from contextlib import ExitStack

import numpy as np

import concourse.bass as bass
from concourse import mybir

ALU = mybir.AluOpType
ACT = mybir.ActivationFunctionType
AX = mybir.AxisListType
F32 = mybir.dt.float32
F32R = mybir.dt.float32r
BF16 = mybir.dt.bfloat16
I32 = mybir.dt.int32

P = 128
B, N, D = 4, 512, 512
HD = 32
HALF = HD // 2
HG = P // HD
G = D // P
TT = N // P
QKV_G = 3 * P
SPLIT_ROWS = 3 * HD
SHIFT_ROW = SPLIT_ROWS
LN_EPS = 1e-5
RMS_EPS = 1e-6
THETA = 10000.0
NEG = -1e30
FP8_MAX = 448.0
FP8_MIN_NORMAL = 2.0 ** -6
ROUND_4BIT = 1.5 * 2.0 ** 20
EXPONENT_BITS = 0x7F800000
SM_SCALE = 1.0 / float(np.sqrt(HD))

S_UNITS = ([(0, (0, 1, 2, 3))] + [(1, (0, 1)), (1, (2, 3))]
           + [(2, (j,)) for j in range(HG)] + [(3, (j,)) for j in range(HG)])
NS = len(S_UNITS)
ST_UNITS = ([[(j, 0, 0)] for j in range(HG)]
            + [[(j, 1, 0), (j, 3, N - P)] for j in range(HG)]
            + [[(j, 2, 0), (j + 1, 2, N // 2)] for j in (0, 2)])
NST = len(ST_UNITS)
STACKS = 6 * HG
SLOTS = {0: [], 1: [0], 2: [1], 3: [2, 3]}
QUANTS = {0: [0], 1: [1], 2: [2, 3], 3: []}
QC = 8


def rope_tables():
    inv = (np.float32(1.0) / np.power(np.float32(THETA), np.arange(0, HD, 2, dtype=np.float32) / np.float32(HD),
                                      dtype=np.float32)).astype(np.float32)
    freqs = (np.arange(N, dtype=np.float32)[:, None] * inv[None, :]).astype(np.float32)
    cos, sin = np.cos(freqs.astype(np.float64)), np.sin(freqs.astype(np.float64))
    both = np.stack([np.concatenate([cos, cos], 1), np.concatenate([-sin, sin], 1)], 0).astype(np.float32)
    return np.ascontiguousarray(both.reshape(2, TT, P, HD).transpose(2, 0, 1, 3))


def build_program(nc, x, w_qkv, w_out, q_gamma, k_gamma, w_ffn, rope, out):
    with ExitStack() as ctx:
        def sb(name, shape, dt=F32):
            return ctx.enter_context(nc.sbuf_tensor(name, shape, dt))

        def ps(name, shape, dt=F32):
            return ctx.enter_context(nc.psum_tensor(name, shape, dt))

        def sem(name):
            return ctx.enter_context(nc.semaphore(name))

        wqkv_hi = sb("wqkv_hi", [P, G, 3 * D], F32R)
        wqkv_lo = sb("wqkv_lo", [P, G, 3 * D], F32R)
        wout_hi = sb("wout_hi", [P, G, D], F32R)
        wout_lo = sb("wout_lo", [P, G, D], F32R)
        wffn_hi = sb("wffn_hi", [P, G, D], F32R)
        wffn_lo = sb("wffn_lo", [P, G, D], F32R)
        ident = sb("ident", [P, P])
        ident_bf = sb("ident_bf", [P, P], BF16)
        mask_q = sb("mask_q", [P, P], BF16)
        mask_k = sb("mask_k", [P, P], BF16)
        ones = sb("ones", [P, HD])
        wait_v = sb("wait_v", [P, 1])
        wait_p = sb("wait_p", [P, 1])
        half_neg = sb("half_neg", [P, 2 * HG * TT])
        table = sb("table", [P, 2, TT, HD])
        gamma = sb("gamma", [P, 2, HD])
        rope_c = sb("rope_c", [P, 2, TT, HD])
        rope_s = sb("rope_s", [P, 2, TT, HD])
        xh = sb("xh", [P, TT, D])
        ln_st = sb("ln_st", [P, TT, 6])
        ln_mv = sb("ln_mv", [P, TT, 2])
        ln_var = sb("ln_var", [P, TT])
        ln_rs = sb("ln_rs", [P, TT])
        hT_hi = sb("hT_hi", [P, TT, G, P], F32R)
        hT_lo = sb("hT_lo", [P, TT, G, P], F32R)
        qkv = sb("qkv", [P, 2, TT, QKV_G])
        rot = sb("rot", [P, TT, 2 * P])
        tmp = sb("tmp", [P, TT, 2 * P])
        ss = sb("ss", [P, 2 * HG * TT])
        ssv = sb("ssv", [P, 2 * HG * TT])
        rs = sb("rs", [P, 2 * HG * TT])
        qkT_hi = sb("qkT_hi", [P, 2, N], F32R)
        qkT_lo = sb("qkT_lo", [P, 2, N], F32R)
        q_stack = sb("q_stack", [P, HG, N], F32R)
        k_stack = sb("k_stack", [P, HG, N], F32R)
        rowmax = sb("rowmax", [P, 2, HG * TT])
        negmax = sb("negmax", [HG * TT, P], F32R)
        prob = sb("prob", [P, NST, N])
        den_t = sb("den_t", [P, N])
        den_r = sb("den_r", [P, N // HD])
        att = sb("att", [P, N])
        attT_hi = sb("attT_hi", [P, G, N], F32R)
        attT_lo = sb("attT_lo", [P, G, N], F32R)
        x1 = sb("x1", [P, TT, D])
        f_st = sb("f_st", [P, 6])
        f_mv = sb("f_mv", [P, 2])
        f_var = sb("f_var", [P, 1])
        f_rs = sb("f_rs", [P, 1])
        amax = sb("amax", [P, G])
        scl = sb("scl", [P, 2, G])
        rscl = sb("rscl", [P, G])
        y = sb("y", [P, D])
        mag = sb("mag", [P, D])
        q8 = sb("q8", [P, 2, D], BF16)
        q8T = sb("q8T", [P, G, P], F32R)
        acc = sb("acc", [P, 2, D])

        gp = [ps(f"gp{i}", [P, 512]) for i in range(2)]
        sp_ = [ps(f"sp{i}", [P, 512]) for i in range(2)]
        tp = [ps(f"tp{i}", [P, 512]) for i in range(2)]
        pv = ps("pv", [P, 512])
        dn = ps("dn", [P, 512])

        s_wload = [sem(f"w_loaded{i}") for i in range(G)]
        s_tload = sem("tables_loaded")
        s_const = sem("constants_ready")
        s_pool_c = sem("constants_step")
        s_const_v = sem("vector_constants_ready")
        s_fold = sem("tables_folded")
        s_whi = sem("wqkv_hi_ready")
        s_wlo = sem("wqkv_lo_ready")
        s_wout_ld = sem("wout_loaded")
        s_wout_hi = sem("wout_hi_ready")
        s_wout_lo = sem("wout_lo_ready")
        s_wffn_ld = sem("wffn_loaded")
        s_wq = sem("wffn_quant_step")
        s_wq_T = sem("wffn_transposed")
        s_wffn_hi = sem("wffn_hi_ready")
        s_wffn_lo = sem("wffn_lo_ready")
        s_x = sem("x_loaded")
        s_st = sem("ln_stats")
        s_mv = sem("ln_moments")
        s_var = sem("ln_var_eps")
        s_rs = sem("ln_rstd")
        s_h = sem("h_ready")
        s_hT = sem("h_transposed")
        s_hT_hi = sem("hT_hi_ready")
        s_hT_lo = sem("hT_lo_ready")
        s_qkv = sem("qkv_done")
        s_raw = sem("qkv_copied")
        s_sq = sem("squares_ready")
        s_ss = sem("square_sums")
        s_ssv = sem("mean_squares")
        s_rrs = sem("head_rstd")
        s_cos = sem("cos_part")
        s_sin = sem("sin_part")
        s_rsum = sem("rotated")
        s_rope = sem("qk_ready")
        s_qkT = sem("qk_transposed")
        s_qk_hi = sem("qkT_hi_ready")
        s_qk_lo = sem("qkT_lo_ready")
        s_stack = sem("stack_loaded")
        s_S = sem("scores_done")
        s_max = sem("rowmax_ready")
        s_mT = sem("rowmax_transposed")
        s_mneg = sem("negmax_ready")
        s_m = sem("shift_loaded")
        s_T = sem("t_scores_done")
        s_exp = sem("exp_done")
        s_pv = sem("pv_done")
        s_dt = sem("den_transposed")
        s_dr = sem("den_reciprocal")
        s_db = sem("den_broadcast")
        s_att = sem("att_ready")
        s_att_hi = sem("attT_hi_ready")
        s_att_lo = sem("attT_lo_ready")
        s_x1l = sem("residual_loaded")
        s_op = sem("out_proj_done")
        s_x1 = sem("x1_ready")
        s_fst = sem("ffn_ln_step")
        s_frs = sem("ffn_rstd")
        s_q = sem("quant_step")
        s_qT = sem("q8_transposed")
        s_qTc = sem("q8T_ready")
        s_ff = sem("ffn_done")
        s_acc = sem("acc_step")
        s_out = [sem(f"out_stored{i}") for i in range(2)]

        wq_stage = [prob[:, 3 * i:3 * i + 3, :].rearrange("p a n -> p (a n)") for i in range(3)]
        wq_stage.append(x1[:, 0:3, :].rearrange("p a n -> p (a n)"))

        def f(ap):
            return ap.bitcast(F32)

        def batches(eng, body):
            body(0, True, False)
            with eng.Fori(1, B - 1) as b:
                body(b, False, False)
            body(B - 1, False, True)

        block = ctx.enter_context(nc.Block())

        @block.sync
        def _(q):
            x_t = x.rearrange("b (t p) d -> b p t d", p=P)
            out_t = out.rearrange("b (t p) d -> b t p d", p=P)

            def load_x(b):
                q.dma_start(xh[:], x_t[bass.ds(b, 1)].rearrange("o p t d -> p (o t) d")).then_inc(s_x, 16)

            def stack(s):
                if not (isinstance(s, int) and s == 0):
                    q.wait_ge(s_T, NST * s)
                for i, (dst, part) in enumerate(((q_stack, (qkT_hi, qkT_hi, qkT_lo)),
                                                 (k_stack, (qkT_hi, qkT_lo, qkT_hi)))):
                    q.wait_ge(s_qk_lo, 2 * s + i + 1)
                    for r in range(3):
                        for j in range(HG):
                            q.dma_start(f(dst[r * HD:(r + 1) * HD, j, :]),
                                        f(part[r][j * HD:(j + 1) * HD, i, :])).then_inc(s_stack, 16)

            def store(p, tiles):
                for t in tiles:
                    q.wait_ge(s_acc, G * (4 * p + t + 1))
                    q.dma_start(out_t[bass.ds(p, 1), t].rearrange("o p d -> p (o d)"),
                                acc[:, t % 2, :]).then_inc(s_out[t % 2], 16)

            q.dma_start(xh[:], x_t[0]).then_inc(s_x, 16)
            for i in range(G):
                q.dma_start(wq_stage[i], w_qkv[i * P:(i + 1) * P, :]).then_inc(s_wload[i], 16)
            q.dma_start(table[:], rope).then_inc(s_tload, 16)
            q.dma_start(gamma[:, 0, :], q_gamma.rearrange("(o n) -> o n", o=1).to_broadcast([P, HD])).then_inc(s_tload, 16)
            q.dma_start(gamma[:, 1, :], k_gamma.rearrange("(o n) -> o n", o=1).to_broadcast([P, HD])).then_inc(s_tload, 16)
            stack(0)
            q.wait_ge(s_wlo, G)
            q.dma_start(x1[:], w_out.rearrange("(g p) n -> p g n", p=P)).then_inc(s_wout_ld, 16)

            def body(b, first, last):
                for hg in range(G):
                    s = 4 * b + hg
                    if hg == 0 and not last:
                        q.wait_ge(s_hT, TT * (b + 1))
                        load_x(b + 1)
                    q.wait_ge(s_mneg, s + 1)
                    q.dma_start(f(q_stack[SHIFT_ROW:SHIFT_ROW + 1, :, :]),
                                f(negmax[:])).then_inc(s_m, 16)
                    if first and hg == 0:
                        q.wait_ge(s_wout_lo, 1)
                        q.dma_start(x1[:], w_ffn.rearrange("(t p) n -> p t n", p=P)).then_inc(s_wffn_ld, 16)
                    if not first:
                        store(b - 1, SLOTS[hg])
                    if hg == 3:
                        if first:
                            q.wait_ge(s_wq_T, G)
                        else:
                            q.wait_ge(s_acc, G * TT * b)
                        q.dma_start(x1[:], x_t[bass.ds(b, 1)].rearrange("o p t d -> p (o t) d")).then_inc(s_x1l, 16)
                    if not (last and hg == 3):
                        stack(s + 1)

            batches(q, body)
            store(B - 1, range(TT))
            for i in range(2):
                q.wait_ge(s_out[i], 16 * (1 + B * TT // 2))

        @block.tensor
        def _(pe):
            def split_product(dst, a_hi, a_lo, w_hi, w_lo, n):
                for i in range(n):
                    pe.matmul(dst, a_hi(i), w_hi(i), start=(i == 0), stop=False)
                    pe.matmul(dst, a_hi(i), w_lo(i), start=False, stop=False)
                    mm = pe.matmul(dst, a_lo(i), w_hi(i), start=False, stop=(i == n - 1))
                return mm

            def banks_free(s):
                pe.wait_ge(s_mneg, s + 1)
                pe.wait_ge(s_raw, min(TT * (s + 2), TT * G * B) if isinstance(s, int) else TT * (s + 2))

            def transpose_h(b, t):
                pe.wait_ge(s_h, TT * b + t + 1)
                if t >= 2:
                    pe.wait_ge(s_hT_lo, TT * b + t - 1)
                for g in range(G):
                    mm = pe.transpose(gp[t % 2][:, g * P:(g + 1) * P], xh[:, t, g * P:(g + 1) * P], ident[:])
                mm.then_inc(s_hT, 1)

            def project(s, b, hg, t):
                pe.wait_ge(s_hT_lo, TT * b + t + 1)
                if t >= 2:
                    pe.wait_ge(s_raw, TT * s + t - 1)
                else:
                    if isinstance(s, int) and s == 0:
                        pe.wait_ge(s_hT_lo, TT - 1 + t)
                    else:
                        pe.wait_ge(s_qk_lo, 2 * (s - 1) + 1 + t)

                def w(part):
                    def cols(i):
                        return part[:, i, :].rearrange("p (c n) -> p c n", c=3)[:, :, hg * P:(hg + 1) * P]
                    return cols
                split_product(gp[t % 2][:, 0:QKV_G], lambda i: hT_hi[:, t, i, :], lambda i: hT_lo[:, t, i, :],
                              w(wqkv_hi), w(wqkv_lo), G).then_inc(s_qkv, 1)

            def transpose_qk(s):
                pe.wait_ge(s_rope, s + 1)
                for i in range(2):
                    for t in range(TT):
                        mm = pe.transpose(gp[i][:, t * P:(t + 1) * P], rot[:, t, i * P:(i + 1) * P], ident[:])
                    mm.then_inc(s_qkT, 1)

            def scores(s, hg, u):
                t, heads = S_UNITS[u]
                if u == 0:
                    pe.wait_ge(s_stack, 16 * STACKS * (s + 1))
                if not (isinstance(s, int) and s == 0 and u < 2):
                    pe.wait_ge(s_max, NS * s + u - 1)
                bank = sp_[(NS * hg + u) % 2]
                width = (t + 1) * P
                for i, j in enumerate(heads):
                    lo = i * width
                    pe.matmul(bank[:, lo + t * P:lo + width], ident_bf[:], mask_q[:], start=True, stop=False,
                              skip_group_check=True)
                    mm = pe.matmul(bank[:, lo:lo + width], q_stack[0:SPLIT_ROWS, j, t * P:(t + 1) * P],
                                   k_stack[0:SPLIT_ROWS, j, 0:width], start=False, stop=True,
                                   skip_group_check=True)
                mm.then_inc(s_S, 1)

            def transpose_max(s, hg, after_qkv):
                pe.wait_ge(s_max, NS * (s + 1))
                if after_qkv:
                    pe.wait_ge(s_raw, TT * (s + 1) + 3)
                else:
                    pe.wait_ge(s_qk_lo, 2 * s + 2)
                pe.transpose(gp[0][0:HG * TT, 0:P], rowmax[:, hg % 2, :], ident[:]).then_inc(s_mT, 1)

            def t_scores(s, v):
                if v == 0:
                    pe.wait_ge(s_m, 16 * (s + 1))
                if not (isinstance(s, int) and s == 0 and v < 2):
                    pe.wait_ge(s_exp, NST * s + v - 1)
                bank = tp[v % 2]
                for j, kt, lo in ST_UNITS[v]:
                    width = N - kt * P
                    pe.matmul(bank[:, lo:lo + P], ident_bf[:], mask_k[:], start=True, stop=False,
                              skip_group_check=True)
                    mm = pe.matmul(bank[:, lo:lo + width], k_stack[0:SHIFT_ROW + 1, j, kt * P:(kt + 1) * P],
                                   q_stack[0:SHIFT_ROW + 1, j, kt * P:N], start=False, stop=True,
                                   skip_group_check=True)
                mm.then_inc(s_T, 1)

            def attend(s, hg, units, need, first_chunk, last_chunk):
                pe.wait_ge(s_exp, NST * s + need)
                if first_chunk and not (isinstance(s, int) and s == 0):
                    pe.wait_ge(s_att, s)
                by_kt = {}
                for v in units:
                    for j, kt, lo in ST_UNITS[v]:
                        by_kt.setdefault(kt, []).append((v, j, lo))
                for dst, val in ((pv, True), (dn, False)):
                    for n, (kt, parts) in enumerate(by_kt.items()):
                        for v, j, lo in parts:
                            c = slice(j * HD, (j + 1) * HD)
                            lhs = qkv[:, hg % 2, kt, 2 * P + j * HD:2 * P + (j + 1) * HD] if val else ones[:]
                            mm = pe.matmul(dst[c, kt * P:N], lhs, prob[:, v, lo:lo + N - kt * P],
                                           start=(kt == 0), stop=(last_chunk and n == len(by_kt) - 1),
                                           skip_group_check=True)
                mm.then_inc(s_pv, 1)

            def out_proj(p, t, s):
                if t == 0:
                    pe.wait_ge(s_att_lo, G * (p + 1))
                    pe.wait_ge(s_wout_lo, 1)
                    banks_free(s)
                if t >= 2:
                    pe.wait_ge(s_x1, TT * p + t - 1)
                cols = slice(t * P, (t + 1) * P)
                split_product(gp[t % 2][:], lambda i: attT_hi[:, i, cols], lambda i: attT_lo[:, i, cols],
                              lambda i: wout_hi[:, i, :], lambda i: wout_lo[:, i, :], G).then_inc(s_op, 1)

            def ffn(p, t, s, first_in_slot):
                n = TT * p + t
                pe.wait_ge(s_q, QC * (n + 1))
                if first_in_slot:
                    banks_free(s)
                else:
                    pe.wait_ge(s_acc, G * n)
                for g in range(G):
                    mm = pe.transpose(gp[0][:].bitcast(BF16)[:, g * P:(g + 1) * P], q8[:, t % 2, g * P:(g + 1) * P], ident_bf[:])
                mm.then_inc(s_qT, 1)
                pe.wait_ge(s_qTc, n + 1)
                for g in range(G):
                    if g == 0 and t == 0:
                        pe.wait_ge(s_wffn_lo, G)
                    if g >= 2:
                        pe.wait_ge(s_acc, G * n + g - 1)
                    bank = gp[(g + 1) % 2]
                    pe.matmul(bank[:], q8T[:, g, :], wffn_hi[:, g, :], start=True, stop=False)
                    pe.matmul(bank[:], q8T[:, g, :], wffn_lo[:, g, :], start=False, stop=True).then_inc(s_ff, 1)

            def transpose_wffn(t):
                pe.wait_ge(s_wq, (QC + 1) * (t + 1))
                if t == 0:
                    banks_free(1)
                if t >= 2:
                    pe.wait_ge(s_wffn_lo, t - 1)
                for g in range(G):
                    mm = pe.transpose(gp[t % 2][:, g * P:(g + 1) * P], x1[:, t, g * P:(g + 1) * P], ident[:])
                mm.then_inc(s_wq_T, 1)

            def body(b, first, last):
                for hg in range(G):
                    s = 4 * b + hg
                    more = not (last and hg == 3)
                    nb, nhg = (b, hg + 1) if hg < 3 else (b + 1, 0)
                    u = 0
                    for t in range(TT):
                        if more:
                            project(s + 1, nb, nhg, t)
                        for _ in range(3 if t < 3 else NS - 9):
                            scores(s, hg, u)
                            u += 1
                    transpose_max(s, hg, more)
                    if hg == 0 and not first:
                        for t in range(TT):
                            out_proj(b - 1, t, s)
                    if not first:
                        for i, t in enumerate(SLOTS[hg]):
                            ffn(b - 1, t, s, i == 0)
                    if first and hg == 1:
                        for t in range(TT):
                            transpose_wffn(t)
                    if hg == 2 and not last:
                        banks_free(s)
                        if not first:
                            pe.wait_ge(s_acc, G * (TT * (b - 1) + 2))
                        for t in range(TT):
                            transpose_h(b + 1, t)
                    for v in range(6):
                        t_scores(s, v)
                    attend(s, hg, range(0, 4), 4, True, False)
                    for v in range(6, 8):
                        t_scores(s, v)
                    if more:
                        banks_free(s)
                        if not first:
                            if hg == 0:
                                pe.wait_ge(s_x1, TT * b)
                            else:
                                pe.wait_ge(s_acc, G * (TT * (b - 1) + SLOTS[hg][-1] + 1))
                        elif hg == 1:
                            pe.wait_ge(s_wffn_lo, G)
                        if hg == 2 and not last:
                            pe.wait_ge(s_hT_lo, TT * (b + 2))
                        transpose_qk(s + 1)
                    for v in range(8, 10):
                        t_scores(s, v)
                    attend(s, hg, range(4, 8), 8, False, False)
                    attend(s, hg, range(8, 10), 10, False, True)

            pe.wait_ge(s_const, 1)
            for t in range(TT):
                transpose_h(0, t)
            pe.wait_ge(s_wlo, G)
            for t in range(TT):
                project(0, 0, 0, t)
            pe.wait_ge(s_raw, TT)
            transpose_qk(0)
            pe.wait_ge(s_const_v, 1)
            batches(pe, body)
            last = G * B - 1
            for t in range(TT):
                out_proj(B - 1, t, last)
            for t in range(TT):
                if t == 0:
                    pe.wait_ge(s_x1, TT * B)
                ffn(B - 1, t, last, t == 0)

        @block.scalar
        def _(act):
            def h_hi(b, t):
                act.wait_ge(s_hT, TT * b + t + 1)
                if t == 0 and not (isinstance(b, int) and b == 0):
                    act.wait_ge(s_qkv, TT * G * b)
                act.copy(hT_hi[:, t, :, :].rearrange("p g n -> p (g n)"), gp[t % 2][:]).then_inc(s_hT_hi, 1)

            def copy_qkv(s, nhg):
                for t in range(TT):
                    act.wait_ge(s_qkv, TT * s + t + 1)
                    if t == 0 and not (isinstance(s, int) and s < 2):
                        act.wait_ge(s_pv, 3 * (s - 1))
                    act.copy(qkv[:, nhg % 2, t, :], gp[t % 2][:, 0:QKV_G]).then_inc(s_raw, 1)
                act.wait_ge(s_raw, TT * (s + 1))
                if not (isinstance(s, int) and s == 0):
                    act.wait_ge(s_rsum, s)
                act.activation(tmp[:], qkv[:, nhg % 2, :, 0:2 * P], ACT.Square).then_inc(s_sq, 1)

            def qk_hi(s):
                for i in range(2):
                    act.wait_ge(s_qkT, 2 * s + i + 1)
                    if i == 0 and not (isinstance(s, int) and s == 0):
                        act.wait_ge(s_stack, 16 * STACKS * s)
                    act.copy(qkT_hi[:, i, :], gp[i][:]).then_inc(s_qk_hi, 1)

            def exps(s, units):
                for v in units:
                    act.wait_ge(s_T, NST * s + v + 1)
                    if not (isinstance(s, int) and s == 0) and v in (0, 4, 8):
                        act.wait_ge(s_pv, 3 * (s - 1) + v // 4 + 1)
                    act.activation(prob[:, v, :], tp[v % 2][:], ACT.Exp, scale=SM_SCALE).then_inc(s_exp, 1)

            def q8_copy(n):
                act.wait_ge(s_qT, 2 + n + 1)
                act.copy(q8T[:].rearrange("p g n -> p (g n)"), gp[0][:].bitcast(BF16)[:, 0:D]).then_inc(s_qTc, 1)

            def body(b, first, last):
                for hg in range(G):
                    s = 4 * b + hg
                    more = not (last and hg == 3)
                    if more:
                        copy_qkv(s + 1, (hg + 1) % G)
                    act.wait_ge(s_mT, s + 1)
                    if not (first and hg == 0):
                        act.wait_ge(s_m, 16 * s)
                    act.mul(negmax[:], gp[0][0:HG * TT, 0:P], -1.0).then_inc(s_mneg, 1)
                    if first and hg == 0:
                        act.wait_ge(s_wout_ld, 16)
                        act.copy(wout_hi[:], x1[:]).then_inc(s_wout_hi, 1)
                    if first and hg == 1:
                        for t in range(TT):
                            act.wait_ge(s_wq_T, t + 1)
                            act.copy(wffn_hi[:, :, t * P:(t + 1) * P],
                                     gp[t % 2][:].rearrange("p (g n) -> p g n", g=G)).then_inc(s_wffn_hi, 1)
                    if not first:
                        for t in SLOTS[hg]:
                            q8_copy(TT * (b - 1) + t)
                    if hg == 2 and not last:
                        for t in range(TT):
                            h_hi(b + 1, t)
                    exps(s, range(8))
                    if more:
                        qk_hi(s + 1)
                    exps(s, range(8, 10))

            for t in range(TT):
                h_hi(0, t)
            for i in range(G):
                act.wait_ge(s_wload[i], 16)
                act.copy(wqkv_hi[:, i, :], wq_stage[i]).then_inc(s_whi, 1)
            copy_qkv(0, 0)
            qk_hi(0)
            act.wait_ge(s_wlo, G)
            batches(act, body)
            for t in range(TT):
                q8_copy(TT * (B - 1) + t)

        @block.vector
        def _(dve):
            def ln_stats(b):
                dve.wait_ge(s_x, 16 * (b + 1))
                for t in range(TT):
                    dve.bn_stats(ln_st[:, t, :], xh[:, t, :]).then_inc(s_st, 1)
                dve.wait_ge(s_st, TT * (b + 1))
                dve.tensor_copy(wait_v[:], ones[:, 0:1])
                for t in range(TT):
                    dve.bn_aggr(ln_mv[:, t, :], ln_st[:, t, :]).then_inc(s_mv, 1)
                dve.wait_ge(s_mv, TT * (b + 1))
                dve.tensor_scalar(ln_var[:], ln_mv[:, :, 1], LN_EPS, None, ALU.add).then_inc(s_var, 1)

            def ln_apply(b):
                dve.wait_ge(s_rs, b + 1)
                for t in range(TT):
                    dve.tensor_scalar(xh[:, t, :], xh[:, t, :], ln_mv[:, t, 0:1], ln_rs[:, t:t + 1],
                                      ALU.subtract, ALU.mult).then_inc(s_h, 1)

            def h_lo(b):
                for t in range(TT):
                    dve.wait_ge(s_hT_hi, TT * b + t + 1)
                    dve.tensor_tensor(hT_lo[:, t, :, :].rearrange("p g n -> p (g n)"), gp[t % 2][:],
                                      f(hT_hi[:, t, :, :]).rearrange("p g n -> p (g n)"),
                                      ALU.subtract).then_inc(s_hT_lo, 1)

            def rotate(s, nhg):
                raw = qkv[:, nhg % 2, :, 0:2 * P].rearrange("p t (i j n) -> p t i j n", i=2, j=HG)
                t4 = tmp[:].rearrange("p t (i j n) -> p t i j n", i=2, j=HG)
                dve.wait_ge(s_sq, s + 1)
                dve.tensor_reduce(ss[:], tmp[:].rearrange("p t (h n) -> p (t h) n", n=HD), AX.X, ALU.add).then_inc(s_ss, 1)
                dve.wait_ge(s_ss, s + 1)
                dve.tensor_scalar(ssv[:], ss[:], 1.0 / HD, RMS_EPS, ALU.mult, ALU.add).then_inc(s_ssv, 1)
                for i in range(2):
                    for h in range(2):
                        src = raw[:, :, i, :, (1 - h) * HALF:(2 - h) * HALF]
                        sin = rope_s[:, i, :, h * HALF:(h + 1) * HALF].unsqueeze(2).to_broadcast([P, TT, HG, HALF])
                        dve.tensor_tensor(t4[:, :, i, :, h * HALF:(h + 1) * HALF], src, sin, ALU.mult).then_inc(s_sin, 1)
                dve.wait_ge(s_sin, 4 * (s + 1))
                dve.wait_ge(s_cos, 2 * (s + 1))
                dve.tensor_tensor(rot[:], rot[:], tmp[:], ALU.add).then_inc(s_rsum, 1)
                dve.wait_ge(s_rsum, s + 1)
                dve.wait_ge(s_rrs, s + 1)
                r = rot[:].rearrange("p t (h n) -> p (t h) n", n=HD)
                dve.tensor_tensor(r, r, rs[:].unsqueeze(2).to_broadcast([P, 2 * HG * TT, HD]), ALU.mult).then_inc(s_rope, 1)

            def qk_lo(s):
                for i in range(2):
                    dve.wait_ge(s_qk_hi, 2 * s + i + 1)
                    dve.tensor_tensor(qkT_lo[:, i, :], gp[i][:], f(qkT_hi[:, i, :]), ALU.subtract).then_inc(s_qk_lo, 1)

            def row_max(s, hg):
                if not (isinstance(s, int) and s < 2):
                    dve.wait_ge(s_mT, s - 1)
                m = rowmax[:, hg % 2, :].rearrange("p (j t) -> p j t", t=TT)
                for u, (t, heads) in enumerate(S_UNITS):
                    dve.wait_ge(s_S, NS * s + u + 1)
                    w = (t + 1) * P
                    src = sp_[(NS * hg + u) % 2][:, 0:w * len(heads)].rearrange("p (j n) -> p j n", n=w)
                    dve.tensor_reduce(m[:, heads[0]:heads[-1] + 1, t], src, AX.X, ALU.max).then_inc(s_max, 1)

            def normalise(s):
                dve.wait_ge(s_pv, 3 * (s + 1))
                dve.transpose(den_t[:], dn[:]).then_inc(s_dt, 1)
                dve.wait_ge(s_dt, s + 1)
                dve.reciprocal(den_r[:], den_t[:].rearrange("p (c n) -> p c n", n=HD)[:, :, 0]).then_inc(s_dr, 1)
                dve.wait_ge(s_dr, s + 1)
                dve.transpose(den_t[:], den_r[:].unsqueeze(2).to_broadcast([P, N // HD, HD])).then_inc(s_db, 1)
                dve.wait_ge(s_db, s + 1)
                if not (isinstance(s, int) and s == 0):
                    dve.wait_ge(s_att_lo, s)
                dve.tensor_tensor(att[:], pv[:], den_t[:], ALU.mult).then_inc(s_att, 1)

            def quantise(src, scale, out_q, done, at, free):
                k = [0]

                def link(ins):
                    k[0] += 1
                    ins.then_inc(done, 1)
                    dve.wait_ge(done, at + k[0])
                blk = src.rearrange("p (g n) -> p g n", g=G)
                link(dve.tensor_reduce(amax[:], blk, AX.X, ALU.max, apply_absolute_value=True))
                link(dve.tensor_scalar(scale, amax[:], 1.0 / FP8_MAX, None, ALU.mult))
                link(dve.reciprocal(rscl[:], scale))
                link(dve.tensor_tensor(y[:].rearrange("p (g n) -> p g n", g=G), blk,
                                       rscl[:].unsqueeze(2).to_broadcast([P, G, P]), ALU.mult))
                link(dve.tensor_scalar(mag[:].bitcast(I32), y[:].bitcast(I32), EXPONENT_BITS, None, ALU.bitwise_and))
                link(dve.tensor_scalar(mag[:], mag[:], FP8_MIN_NORMAL, ROUND_4BIT, ALU.max, ALU.mult))
                k[0] += 1
                dve.tensor_tensor(y[:], y[:], mag[:], ALU.add).then_inc(done, 1)
                dve.wait_ge(done, at + k[0])
                if free is not None:
                    free()
                dve.tensor_tensor(out_q, y[:], mag[:], ALU.subtract).then_inc(done, 1)

            def ffn_quant(p, t):
                n = TT * p + t
                src = x1[:, t, :]
                if t == 0:
                    dve.wait_ge(s_x1, TT * (p + 1))
                dve.bn_stats(f_st[:], src).then_inc(s_fst, 1)
                dve.wait_ge(s_fst, 4 * n + 1)
                dve.tensor_copy(wait_v[:], ones[:, 0:1])
                dve.bn_aggr(f_mv[:], f_st[:]).then_inc(s_fst, 1)
                dve.wait_ge(s_fst, 4 * n + 2)
                dve.tensor_scalar(f_var[:], f_mv[:, 1:2], LN_EPS, None, ALU.add).then_inc(s_fst, 1)
                dve.wait_ge(s_frs, n + 1)
                dve.tensor_scalar(y[:], src, f_mv[:, 0:1], f_rs[:], ALU.subtract, ALU.mult).then_inc(s_fst, 1)
                dve.wait_ge(s_fst, 4 * n + 4)

                def free():
                    dve.wait_ge(s_qT, n + 1)
                quantise(y[:], scl[:, t % 2, :], q8[:, t % 2, :], s_q, QC * n, free)

            def ffn_sum(p, t):
                n = TT * p + t
                dve.wait_ge(s_out[t % 2], 16 * (1 + TT // 2 * p + t // 2))
                for g in range(G):
                    dve.wait_ge(s_ff, G * n + g + 1)
                    if g:
                        dve.wait_ge(s_acc, G * n + g)
                    a = acc[:, t % 2, :]
                    dve.scalar_tensor_tensor(out=a, in0=gp[(g + 1) % 2][:], scalar=scl[:, t % 2, g:g + 1],
                                             in1=x1[:, t, :] if g == 0 else a,
                                             op0=ALU.mult, op1=ALU.add).then_inc(s_acc, 1)

            def out_sum(p):
                dve.wait_ge(s_x1l, 16 * (p + 1))
                for t in range(TT):
                    dve.wait_ge(s_op, TT * p + t + 1)
                    dve.tensor_tensor(x1[:, t, :], gp[t % 2][:], x1[:, t, :], ALU.add).then_inc(s_x1, 1)

            def wffn_quant():
                dve.wait_ge(s_wffn_ld, 16)
                for t in range(TT):
                    src = x1[:, t, :]
                    quantise(src, scl[:, 0, :], y[:], s_wq, (QC + 1) * t, None)
                    dve.wait_ge(s_wq, (QC + 1) * t + QC)
                    dve.tensor_tensor(src.rearrange("p (g n) -> p g n", g=G), y[:].rearrange("p (g n) -> p g n", g=G),
                                      scl[:, 0, :].unsqueeze(2).to_broadcast([P, G, P]), ALU.mult).then_inc(s_wq, 1)
                    dve.wait_ge(s_wq, (QC + 1) * (t + 1))

            def wffn_split():
                for t in range(TT):
                    dve.wait_ge(s_wffn_hi, t + 1)
                    cols = slice(t * P, (t + 1) * P)
                    dve.tensor_tensor(wffn_lo[:, :, cols], gp[t % 2][:].rearrange("p (g n) -> p g n", g=G),
                                      f(wffn_hi[:, :, cols]), ALU.subtract).then_inc(s_wffn_lo, 1)

            def body(b, first, last):
                for hg in range(G):
                    s = 4 * b + hg
                    more = not (last and hg == 3)
                    row_max(s, hg)
                    if more:
                        rotate(s + 1, (hg + 1) % G)
                    if first and hg == 0:
                        dve.wait_ge(s_wout_hi, 1)
                        dve.tensor_tensor(wout_lo[:], x1[:], f(wout_hi[:]), ALU.subtract).then_inc(s_wout_lo, 1)
                    if first and hg == 1:
                        wffn_quant()
                        wffn_split()
                    if not first:
                        if hg == 0:
                            out_sum(b - 1)
                        for t in SLOTS[hg]:
                            ffn_sum(b - 1, t)
                    if hg == 1 and not last:
                        ln_stats(b + 1)
                    if not first:
                        for t in QUANTS[hg][:1]:
                            ffn_quant(b - 1, t)
                    if hg == 1 and not last:
                        ln_apply(b + 1)
                    if hg == 2 and not last:
                        h_lo(b + 1)
                    if not first:
                        for t in QUANTS[hg][1:]:
                            ffn_quant(b - 1, t)
                    if more:
                        qk_lo(s + 1)
                    normalise(s)

            dve.memset(ones[:], 1.0).then_inc(s_const_v, 1)
            dve.wait_ge(s_const_v, 1)
            for i in range(2):
                dve.memset(q8[:, i, 0:2], 0.0).then_inc(s_qT, 1)
                dve.memset(acc[:, i, 0:1], 0.0).then_inc(s_out[i], 16)
            ln_stats(0)
            ln_apply(0)
            h_lo(0)
            for i in range(G):
                dve.wait_ge(s_whi, i + 1)
                dve.tensor_tensor(wqkv_lo[:, i, :], wq_stage[i], f(wqkv_hi[:, i, :]), ALU.subtract).then_inc(s_wlo, 1)
            dve.wait_ge(s_tload, 48)
            for i in range(2):
                dve.tensor_tensor(rope_c[:, i], table[:, 0], gamma[:, i, :].unsqueeze(1).to_broadcast([P, TT, HD]),
                                  ALU.mult).then_inc(s_fold, 1)
                for h in range(2):
                    dve.tensor_tensor(rope_s[:, i, :, h * HALF:(h + 1) * HALF], table[:, 1, :, h * HALF:(h + 1) * HALF],
                                      gamma[:, i, (1 - h) * HALF:(2 - h) * HALF].unsqueeze(1).to_broadcast([P, TT, HALF]),
                                      ALU.mult).then_inc(s_fold, 1)
            dve.wait_ge(s_fold, 6)
            rotate(0, 0)
            qk_lo(0)
            batches(dve, body)
            p = B - 1
            out_sum(p)
            ffn_quant(p, 0)
            for t in range(TT):
                if t + 1 < TT:
                    ffn_quant(p, t + 1)
                ffn_sum(p, t)

        @block.gpsimd
        def _(pool):
            def power(dst, src, done):
                pool.tensor_tensor(dst, src, half_neg[:, 0:src.shape[-1]], ALU.pow).then_inc(done, 1)

            def rotate(s, nhg):
                raw = qkv[:, nhg % 2, :, 0:2 * P].rearrange("p t (i j n) -> p t i j n", i=2, j=HG)
                r = rot[:].rearrange("p t (i j n) -> p t i j n", i=2, j=HG)
                pool.wait_ge(s_raw, TT * (s + 1))
                if not (isinstance(s, int) and s == 0):
                    pool.wait_ge(s_qkT, 2 * s)
                for i in range(2):
                    cos = rope_c[:, i, :, :].unsqueeze(2).to_broadcast([P, TT, HG, HD])
                    pool.tensor_tensor(r[:, :, i], raw[:, :, i], cos, ALU.mult).then_inc(s_cos, 1)
                pool.wait_ge(s_ssv, s + 1)
                if not (isinstance(s, int) and s == 0):
                    pool.wait_ge(s_rope, s)
                power(rs[:], ssv[:], s_rrs)

            def split_att(s, hg, b):
                pool.wait_ge(s_att, s + 1)
                if hg == 0 and not (isinstance(b, int) and b == 0):
                    pool.wait_ge(s_op, TT * b)
                pool.tensor_tensor(wait_p[:], half_neg[:, 0:1], half_neg[:, 0:1], ALU.add)
                pool.tensor_copy(attT_hi[:, hg, :], att[:]).then_inc(s_att_hi, 1)
                pool.wait_ge(s_att_hi, s + 1)
                pool.tensor_tensor(attT_lo[:, hg, :], att[:], f(attT_hi[:, hg, :]), ALU.subtract).then_inc(s_att_lo, 1)

            def ln_power(b):
                pool.wait_ge(s_var, b + 1)
                power(ln_rs[:], ln_var[:], s_rs)

            def ffn_power(p, t):
                n = TT * p + t
                pool.wait_ge(s_fst, 4 * n + 3)
                power(f_rs[:], f_var[:], s_frs)

            def body(b, first, last):
                for hg in range(G):
                    s = 4 * b + hg
                    if not (last and hg == 3):
                        rotate(s + 1, (hg + 1) % G)
                    if hg == 1 and not last:
                        ln_power(b + 1)
                    if not first:
                        for t in QUANTS[hg]:
                            ffn_power(b - 1, t)
                    split_att(s, hg, b)

            def step(ins, count=[0]):
                count[0] += 1
                ins.then_inc(s_pool_c, 1)
                pool.wait_ge(s_pool_c, count[0])

            step(pool.memset(half_neg[:], -0.5))
            ln_power(0)
            step(pool.memset(ident[:], 0.0))
            step(pool.affine_select(ident[:], ident[:], pattern=[[-1, P]], compare_op=ALU.not_equal, fill=1.0,
                                    base=0, channel_multiplier=1))
            step(pool.tensor_copy(ident_bf[:], ident[:]))
            step(pool.memset(mask_q[:], 0.0))
            step(pool.affine_select(mask_q[:], mask_q[:], pattern=[[-1, P]], compare_op=ALU.is_ge, fill=NEG,
                                    base=0, channel_multiplier=1))
            step(pool.memset(mask_k[:], 0.0))
            step(pool.memset(f(k_stack[SHIFT_ROW:SHIFT_ROW + HD, :, :]), 1.0))
            pool.affine_select(mask_k[:], mask_k[:], pattern=[[1, P]], compare_op=ALU.is_ge, fill=NEG,
                               base=0, channel_multiplier=-1).then_inc(s_const, 1)
            pool.wait_ge(s_fold, 6)
            rotate(0, 0)
            batches(pool, body)
            for t in range(TT):
                ffn_power(B - 1, t)


_NAMES = ["L0_attn_x", "L0_attn_w_qkv", "L0_attn_w_out", "L0_attn_q_gamma", "L0_attn_k_gamma", "L0_ffn_weight"]


def kernel(**inputs):
    import numpy as _np
    import concourse.bacc as _bacc
    from concourse import mybir as _mybir
    from concourse.bass_utils import run_bass_kernel_spmd as _run

    nc = _bacc.Bacc("TRN2", target_bir_lowering=False, num_devices=1, dynamic_dma_scratch_size=2048)
    arrays = {f"in_{n}": _np.ascontiguousarray(inputs[n]) for n in _NAMES}
    arrays["in_rope"] = rope_tables()
    args = [nc.dram_tensor(n, a.shape, _mybir.dt.from_np(a.dtype), kind="ExternalInput").ap() for n, a in arrays.items()]
    args.append(nc.dram_tensor("out_0", (B, N, D), _mybir.dt.float32, kind="ExternalOutput").ap())
    build_program(nc, *args)
    r = _run(nc, [arrays], core_ids=[0])
    return r.results[0]["out_0"]
```

```python
from contextlib import ExitStack

import numpy as np

import concourse.bass as bass
from concourse import mybir

ALU = mybir.AluOpType
ACT = mybir.ActivationFunctionType
AX = mybir.AxisListType
F32 = mybir.dt.float32
F32R = mybir.dt.float32r
BF16 = mybir.dt.bfloat16
I32 = mybir.dt.int32

P = 128
B, N, D = 4, 512, 512
HD = 32
HALF = HD // 2
HG = P // HD
G = D // P
TT = N // P
QKV_G = 3 * P
SPLIT_ROWS = 3 * HD
SHIFT_ROW = SPLIT_ROWS
LN_EPS = 1e-5
RMS_EPS = 1e-6
THETA = 10000.0
NEG = -1e30
FP8_MAX = 448.0
FP8_MIN_NORMAL = 2.0 ** -6
ROUND_4BIT = 1.5 * 2.0 ** 20
EXPONENT_BITS = 0x7F800000
SM_SCALE = 1.0 / float(np.sqrt(HD))

S_UNITS = ([(0, (0, 1, 2, 3))] + [(1, (0, 1)), (1, (2, 3))]
           + [(2, (j,)) for j in range(HG)] + [(3, (j,)) for j in range(HG)])
NS = len(S_UNITS)
ST_UNITS = ([[(j, 0, 0)] for j in range(HG)]
            + [[(j, 1, 0), (j, 3, N - P)] for j in range(HG)]
            + [[(j, 2, 0), (j + 1, 2, N // 2)] for j in (0, 2)])
NST = len(ST_UNITS)
STACKS = 6
QC = 8
QC_V = 6
def ffn_bank(t, g):
    return (t % 2 + 1 + g) % 4




def rope_tables():
    inv = (np.float32(1.0) / np.power(np.float32(THETA), np.arange(0, HD, 2, dtype=np.float32) / np.float32(HD),
                                      dtype=np.float32)).astype(np.float32)
    freqs = (np.arange(N, dtype=np.float32)[:, None] * inv[None, :]).astype(np.float32)
    cos, sin = np.cos(freqs.astype(np.float64)), np.sin(freqs.astype(np.float64))
    both = np.stack([np.concatenate([cos, cos], 1), np.concatenate([-sin, sin], 1)], 0).astype(np.float32)
    return np.ascontiguousarray(both.reshape(2, TT, P, HD).transpose(2, 0, 1, 3))


def build_program(nc, x, w_qkv, w_out, q_gamma, k_gamma, w_ffn, rope, out):
    with ExitStack() as ctx:
        def sb(name, shape, dt=F32):
            return ctx.enter_context(nc.sbuf_tensor(name, shape, dt))

        def ps(name, shape, dt=F32):
            return ctx.enter_context(nc.psum_tensor(name, shape, dt))

        def sem(name):
            return ctx.enter_context(nc.semaphore(name))

        wqkv_hi = sb("wqkv_hi", [P, G, 3 * D], F32R)
        wqkv_lo = sb("wqkv_lo", [P, G, 3 * D], F32R)
        wout_hi = sb("wout_hi", [P, G, D], F32R)
        wout_lo = sb("wout_lo", [P, G, D], F32R)
        wffn_hi = sb("wffn_hi", [P, G, D], F32R)
        wffn_lo = sb("wffn_lo", [P, G, D], F32R)
        ident = sb("ident", [P, P])
        ident_bf = sb("ident_bf", [P, P], BF16)
        mask_q = sb("mask_q", [P, P], BF16)
        mask_k = sb("mask_k", [P, P], BF16)
        ones = sb("ones", [P, HD])
        wait_v = sb("wait_v", [P, 1])
        half_neg = sb("half_neg", [P, 2 * HG * TT])
        rope_c = sb("rope_c", [P, 2, TT, HD])
        rope_s = sb("rope_s", [P, 2, TT, HD])
        xh = sb("xh", [P, TT, D])
        ln_st = sb("ln_st", [P, TT, 6])
        ln_mv = sb("ln_mv", [P, TT, 2])
        ln_var = sb("ln_var", [P, TT])
        ln_rs = sb("ln_rs", [P, TT])
        hT_hi = sb("hT_hi", [P, TT, G, P], F32R)
        hT_lo = sb("hT_lo", [P, TT, G, P], F32R)
        qk = sb("qk", [P, TT, 2 * P])
        v = sb("v", [P, G, TT, P])
        rot = sb("rot", [P, TT, 2 * P])
        tmp = sb("tmp", [P, TT, 2 * P])
        ss = sb("ss", [P, 2 * HG * TT])
        ssv = sb("ssv", [P, 2 * HG * TT])
        rs = sb("rs", [P, 2 * HG * TT])
        table = tmp[:, 0, 0:2 * TT * HD].rearrange("p (c t n) -> p c t n", c=2, t=TT)
        gamma = tmp[:, 1, 0:2 * HD].rearrange("p (i n) -> p i n", i=2)
        qkT_hi = sb("qkT_hi", [P, 2, N], F32R)
        qkT_lo = sb("qkT_lo", [P, 2, N], F32R)
        q_stack = sb("q_stack", [P, 2, HG, N], F32R)
        k_stack = sb("k_stack", [P, 2, HG, N], F32R)
        bounce = nc.dram_tensor("bounce", (2, 2, 2, P, N), F32, kind="Internal").ap()
        rowmax = sb("rowmax", [P, 2, HG * TT])
        negmax = sb("negmax", [HG * TT, P], F32R)
        prob = sb("prob", [P, NST, N])
        den_r = sb("den_r", [P, N // HD])
        att = sb("att", [P, N])
        attT_hi = sb("attT_hi", [P, G, N], F32R)
        attT_lo = sb("attT_lo", [P, G, N], F32R)
        x1 = sb("x1", [P, TT, D])
        f_st = sb("f_st", [P, TT, 6])
        f_mv = sb("f_mv", [P, TT, 2])
        f_var = sb("f_var", [P, TT])
        f_rs = sb("f_rs", [P, TT])
        amax = sb("amax", [P, G])
        scl = sb("scl", [P, 2, G])
        rscl = sb("rscl", [P, G])
        y = sb("y", [P, D])
        mag = sb("mag", [P, D])
        q8 = sb("q8", [P, 2, D], BF16)
        q8T = sb("q8T", [P, G, P], F32R)

        gp = [ps(f"gp{i}", [P, 512]) for i in range(2)]
        sp_ = [ps(f"sp{i}", [P, 512]) for i in range(2)]
        tp = [ps(f"tp{i}", [P, 512]) for i in range(2)]
        pv = ps("pv", [P, 512])
        dn = ps("dn", [P, 512])
        slot = gp + sp_

        s_wload = [sem(f"w_loaded{i}") for i in range(G)]
        s_tload = sem("tables_loaded")
        s_const = sem("constants_ready")
        s_ident = sem("identity_ready")
        s_pool_c = sem("constants_step")
        s_const_v = sem("vector_constants_ready")
        s_fold = sem("tables_folded")
        s_whi = sem("wqkv_hi_ready")
        s_wlo = sem("wqkv_lo_ready")
        s_wout_ld = sem("wout_loaded")
        s_wout_hi = sem("wout_hi_ready")
        s_wout_lo = sem("wout_lo_ready")
        s_wffn_ld = sem("wffn_loaded")
        s_wq = sem("wffn_quant_step")
        s_wq_T = sem("wffn_transposed")
        s_wffn_hi = sem("wffn_hi_ready")
        s_wffn_lo = sem("wffn_lo_ready")
        s_x = sem("x_loaded")
        s_st = sem("ln_stats")
        s_mv = sem("ln_moments")
        s_var = sem("ln_var_eps")
        s_rs = sem("ln_rstd")
        s_h = sem("h_ready")
        s_hT = sem("h_transposed")
        s_hT_hi = sem("hT_hi_ready")
        s_hT_lo = sem("hT_lo_ready")
        s_qkv = sem("qkv_done")
        s_raw = sem("qkv_copied")
        s_qk = sem("qk_copied")
        s_sq = sem("squares_ready")
        s_ss = sem("square_sums")
        s_ssv = sem("mean_squares")
        s_rrs = sem("head_rstd")
        s_cos = sem("cos_part")
        s_sin = sem("sin_part")
        s_rsum = sem("rotated")
        s_rope = sem("qk_ready")
        s_qkT = sem("qk_transposed")
        s_qk_hi = sem("qkT_hi_ready")
        s_qk_lo = sem("qkT_lo_ready")
        s_stack = sem("stack_loaded")
        s_S = sem("scores_done")
        s_max = sem("rowmax_ready")
        s_mT = sem("rowmax_transposed")
        s_mneg = sem("negmax_ready")
        s_m = sem("shift_loaded")
        s_T = sem("t_scores_done")
        s_exp = sem("exp_done")
        s_pv = sem("pv_done")
        s_dt = sem("den_transposed")
        s_dr = sem("den_reciprocal")
        s_db = sem("den_broadcast")
        s_att = sem("att_ready")
        s_att_hi = sem("attT_hi_ready")
        s_att_lo = sem("attT_lo_ready")
        s_x1l = sem("residual_loaded")
        s_op = sem("out_proj_done")
        s_x1 = sem("x1_ready")
        s_fst = sem("ffn_ln_step")
        s_h2 = sem("ffn_h_ready")
        s_frs = sem("ffn_rstd")
        s_q = sem("quant_step")
        s_qT = sem("q8_transposed")
        s_qTc = sem("q8T_ready")
        s_ff = sem("ffn_done")
        s_acc = sem("acc_step")
        s_out = sem("out_stored")
        s_bounce = [sem(f"bounce_written{i}") for i in range(2)]

        wq_stage = [prob[:, 3 * i:3 * i + 3, :].rearrange("p a n -> p (a n)") for i in range(3)]
        wq_stage.append(x1[:, 0:3, :].rearrange("p a n -> p (a n)"))
        wffn_stage = [x1[:, 3, :], prob[:, 9, :], att[:], v[:, 3].rearrange("p t n -> p (t n)")]

        def of_groups(w, lo, hi):
            return w.rearrange("p (c n) -> p c n", c=3)[:, :, lo * P:hi * P]

        W_PARTS = ((0, 1), (1, 2), (2, G))

        def f(ap):
            return ap.bitcast(F32)

        def summed(n):
            return n + 1

        def batches(eng, body):
            body(0, True, False)
            with eng.Fori(1, B - 1) as b:
                body(b, False, False)
            body(B - 1, False, True)

        block = ctx.enter_context(nc.Block())

        @block.sync
        def _(q):
            x_t = x.rearrange("b (t p) d -> b p t d", p=P)
            out_t = out.rearrange("b (t p) d -> b t p d", p=P)

            def stack(s, hg):
                for i, (src, ready) in enumerate(((qkT_hi, s_qk_hi), (qkT_lo, s_qk_lo))):
                    q.wait_ge(ready, 2 * (s + 1))
                    q.dma_start(bounce[hg % 2, i].rearrange("c p n -> p c n"), f(src[:])).then_inc(s_bounce[i], 16)
                for r, i in ((0, 0), (1, 0), (2, 0), (2, 1), (1, 1), (0, 1)):
                    part = int((r, i) in ((2, 0), (1, 1)))
                    q.wait_ge(s_bounce[part], 16 * (s + 1))
                    q.dma_start(f((q_stack, k_stack)[i][r * HD:(r + 1) * HD, hg % 2, :, :]),
                                bounce[hg % 2, part, i].rearrange("(j p) n -> p j n", p=HD)).then_inc(s_stack, 16)

            def store(p, tiles):
                for t in tiles:
                    q.wait_ge(s_acc, summed(G * (4 * p + t + 1)))
                    q.dma_start(out_t[bass.ds(p, 1), t].rearrange("o p d -> p (o d)"),
                                x1[:, t, :]).then_inc(s_out, 16)

            q.dma_start(xh[:], x_t[0]).then_inc(s_x, 16)
            for i in range(G):
                q.dma_start(wq_stage[i], w_qkv[i * P:(i + 1) * P, :]).then_inc(s_wload[i], 16)
            q.dma_start(table, rope).then_inc(s_tload, 16)
            q.dma_start(gamma[:, 0, :], q_gamma.rearrange("(o n) -> o n", o=1).to_broadcast([P, HD])).then_inc(s_tload, 16)
            q.dma_start(gamma[:, 1, :], k_gamma.rearrange("(o n) -> o n", o=1).to_broadcast([P, HD])).then_inc(s_tload, 16)
            for t in range(TT):
                q.dma_start(wffn_stage[t], w_ffn[t * P:(t + 1) * P, :]).then_inc(s_wffn_ld, 16)
            stack(0, 0)

            def body(b, first, last):
                for hg in range(G):
                    s = 4 * b + hg
                    if not (last and hg == 3):
                        stack(s + 1, (hg + 1) % G)
                    q.wait_ge(s_mneg, s + 1)
                    q.dma_start(f(q_stack[SHIFT_ROW:SHIFT_ROW + 1, hg % 2, :, :]),
                                f(negmax[:])).then_inc(s_m, 16)
                    if first and hg == 0:
                        q.wait_ge(s_wq_T, G)
                        q.dma_start(x1[:], w_out.rearrange("(g p) n -> p g n", p=P)).then_inc(s_wout_ld, 16)
                    if first and hg == 3:
                        q.wait_ge(s_wout_lo, 1)
                    if hg == 3:
                        if not first:
                            store(b - 1, range(TT))
                            q.wait_ge(s_out, 16 * TT * b)
                        q.dma_start(x1[:], x_t[bass.ds(b, 1)].rearrange("o p t d -> p (o t) d")).then_inc(s_x1l, 16)

            batches(q, body)
            store(B - 1, range(TT))
            q.wait_ge(s_out, 16 * B * TT)

        @block.tensor
        def _(pe):
            def split_product(dst, a_hi, a_lo, w_hi, w_lo, n):
                for i in range(n):
                    pe.matmul(dst, a_hi(i), w_hi(i), start=(i == 0), stop=False)
                    pe.matmul(dst, a_hi(i), w_lo(i), start=False, stop=False)
                    mm = pe.matmul(dst, a_lo(i), w_hi(i), start=False, stop=(i == n - 1))
                return mm

            def banks_free(s):
                pe.wait_ge(s_mneg, s + 1)
                pe.wait_ge(s_raw, min(TT * (s + 3), TT * G * B) if isinstance(s, int) else TT * (s + 3))

            def step_start(b, hg, first, last):
                s = 4 * b + hg
                if first and hg == 0:
                    pe.wait_ge(s_raw, TT * 2)
                    pe.wait_ge(s_wlo, G * len(W_PARTS))
                    return
                banks_free(s - 1)
                if hg == 0:
                    pe.wait_ge(s_acc, summed(G * TT * (b - 1)))
                if hg == 2 and not last:
                    pe.wait_ge(s_hT_lo, TT * (b + 2))
                if hg == 2 and not first:
                    pe.wait_ge(s_x1, TT * b)
                if hg == 1 and first:
                    pe.wait_ge(s_wffn_lo, G)
                if hg == 3 and not first:
                    pe.wait_ge(s_acc, summed(G * (TT * (b - 1) + 2)))

            def transpose_h(b, t):
                pe.wait_ge(s_h, TT * b + t + 1)
                if isinstance(b, int) and b == 0:
                    pass
                elif isinstance(b, int) and b == 1:
                    if t == 0:
                        banks_free(1)
                else:
                    pe.wait_ge(s_x1, TT * (b - 2) + t + 1)
                for g in range(G):
                    mm = pe.transpose(slot[t][:, g * P:(g + 1) * P], xh[:, t, g * P:(g + 1) * P], ident[:])
                mm.then_inc(s_hT, 1)

            def project(s, hg, t, blocks=range(G)):
                if blocks[0] == 0 and t >= 2:
                    pe.wait_ge(s_raw, TT * s + t - 1)
                a_hi, a_lo = hT_hi[:, t], hT_lo[:, t]
                dst = gp[t % 2][:, 0:QKV_G]
                w_hi, w_lo = (w.rearrange("p g (c n) -> p g c n", c=3)[:, :, :, hg * P:(hg + 1) * P]
                              for w in (wqkv_hi[:], wqkv_lo[:]))
                for i in blocks:
                    pe.matmul(dst, a_hi[:, i, :], w_hi[:, i], start=(i == 0), stop=False)
                    pe.matmul(dst, a_hi[:, i, :], w_lo[:, i], start=False, stop=False)
                    mm = pe.matmul(dst, a_lo[:, i, :], w_hi[:, i], start=False, stop=(i == G - 1))
                if blocks[-1] == G - 1:
                    mm.then_inc(s_qkv, 1)

            def transpose_qk(s):
                pe.wait_ge(s_rope, s + 1)
                if not (isinstance(s, int) and s < 2):
                    pe.wait_ge(s_exp, NST * (s - 1))
                for i in range(2):
                    for t in range(TT):
                        mm = pe.transpose(tp[i][:, t * P:(t + 1) * P], rot[:, t, i * P:(i + 1) * P], ident[:])
                    mm.then_inc(s_qkT, 1)

            def scores(s, hg, u):
                t, heads = S_UNITS[u]
                if u == 0:
                    pe.wait_ge(s_stack, 16 * STACKS * (s + 1))
                if not (isinstance(s, int) and s == 0 and u < 2):
                    pe.wait_ge(s_max, NS * s + u - 1)
                bank = sp_[(NS * hg + u) % 2]
                q_st, k_st = q_stack[0:SPLIT_ROWS, hg % 2], k_stack[0:SPLIT_ROWS, hg % 2]
                width = (t + 1) * P
                for i, j in enumerate(heads):
                    lo = i * width
                    pe.matmul(bank[:, lo + t * P:lo + width], ident_bf[:], mask_q[:], start=True, stop=False,
                              skip_group_check=True)
                    mm = pe.matmul(bank[:, lo:lo + width], q_st[:, j, t * P:(t + 1) * P],
                                   k_st[:, j, 0:width], start=False, stop=True,
                                   skip_group_check=True)
                mm.then_inc(s_S, 1)

            def transpose_max(s, hg):
                pe.wait_ge(s_max, NS * (s + 1))
                pe.transpose(sp_[0][0:HG * TT, 0:P], rowmax[:, hg % 2, :], ident[:]).then_inc(s_mT, 1)

            def t_scores(s, hg, v, more1):
                if v == 0:
                    pe.wait_ge(s_m, 16 * (s + 1))
                if v < 2 and more1:
                    pe.wait_ge(s_qk_lo, 2 * (s + 1) + v + 1)
                else:
                    pe.wait_ge(s_exp, NST * s + v - 1)
                bank = tp[v % 2]
                q_st, k_st = q_stack[0:SHIFT_ROW + 1, hg % 2], k_stack[0:SHIFT_ROW + 1, hg % 2]
                for j, kt, lo in ST_UNITS[v]:
                    width = N - kt * P
                    pe.matmul(bank[:, lo:lo + P], ident_bf[:], mask_k[:], start=True, stop=False,
                              skip_group_check=True)
                    mm = pe.matmul(bank[:, lo:lo + width], k_st[:, j, kt * P:(kt + 1) * P],
                                   q_st[:, j, kt * P:N], start=False, stop=True,
                                   skip_group_check=True)
                mm.then_inc(s_T, 1)

            def attend(s, hg, units, need, first_chunk, last_chunk):
                pe.wait_ge(s_exp, NST * s + need)
                if first_chunk and not (isinstance(s, int) and s == 0):
                    pe.wait_ge(s_att, s)
                by_kt = {}
                for u in units:
                    for j, kt, lo in ST_UNITS[u]:
                        by_kt.setdefault(kt, []).append((u, j, lo))
                for dst, val in ((pv, True), (dn, False)):
                    for n, (kt, parts) in enumerate(by_kt.items()):
                        for u, j, lo in parts:
                            c = slice(j * HD, (j + 1) * HD)
                            lhs = v[:, hg, kt, j * HD:(j + 1) * HD] if val else ones[:]
                            mm = pe.matmul(dst[c, kt * P:N], lhs, prob[:, u, lo:lo + N - kt * P],
                                           start=(kt == 0), stop=(last_chunk and n == len(by_kt) - 1),
                                           skip_group_check=True)
                mm.then_inc(s_pv, 1)

            def out_proj(p, t, s):
                if t == 0:
                    pe.wait_ge(s_att_lo, G * (p + 1))
                    banks_free(s)
                cols = slice(t * P, (t + 1) * P)
                split_product(slot[t][:], lambda i: attT_hi[:, i, cols], lambda i: attT_lo[:, i, cols],
                              lambda i: wout_hi[:, i, :], lambda i: wout_lo[:, i, :], G).then_inc(s_op, 1)

            def transpose_q8(p, t, s):
                n = TT * p + t
                pe.wait_ge(s_q, QC * (n + 1))
                if t == 0 or (t == 2 and s is not None):
                    banks_free(s)
                elif t == 2:
                    pe.wait_ge(s_acc, summed(G * (n - 1) + 3))
                else:
                    pe.wait_ge(s_acc, summed(G * (n - 1) + 1))
                for g in range(G):
                    mm = pe.transpose(slot[t % 2][:].bitcast(BF16)[:, g * P:(g + 1) * P],
                                      q8[:, t % 2, g * P:(g + 1) * P], ident_bf[:])
                mm.then_inc(s_qT, 1)

            def ffn(p, t):
                n = TT * p + t
                pe.wait_ge(s_qTc, n + 1)
                for g in range(G):
                    if t % 2 == 1 and g <= 2:
                        pe.wait_ge(s_acc, summed(G * (n - 1) + g + 2))
                    if t == 2 and g == 0:
                        pe.wait_ge(s_acc, summed(G * n))
                    bank = slot[ffn_bank(t, g)]
                    pe.matmul(bank[:], q8T[:, g, :], wffn_hi[:, g, :], start=True, stop=False)
                    pe.matmul(bank[:], q8T[:, g, :], wffn_lo[:, g, :], start=False, stop=True).then_inc(s_ff, 1)

            def transpose_wffn(t):
                pe.wait_ge(s_wq, (QC + 1) * (t + 1))
                if t == 0:
                    banks_free(0)
                for g in range(G):
                    mm = pe.transpose(slot[t][:, g * P:(g + 1) * P], wffn_stage[t][:, g * P:(g + 1) * P], ident[:])
                mm.then_inc(s_wq_T, 1)

            def slot_work(b, hg, k, first, last):
                s = 4 * b + hg
                if hg == 1:
                    if not first:
                        for t in ((0, 1), (2,), (3,), ())[k]:
                            out_proj(b - 1, t, s)
                    if not last:
                        for t in ((), (0,), (1,), (2, 3))[k]:
                            transpose_h(b + 1, t)
                if hg == 0 and first:
                    transpose_wffn(k)
                if hg >= 2 and not first:
                    t = 2 * (hg - 2) + k // 2
                    if k % 2 == 0:
                        transpose_q8(b - 1, t, s)
                    else:
                        ffn(b - 1, t)

            def body(b, first, last):
                for hg in range(G):
                    s = 4 * b + hg
                    more1 = not (last and hg == 3)
                    more2 = not (last and hg >= 2)
                    step_start(b, hg, first, last)
                    for c in range(G * TT):
                        if more2:
                            project(s + 2, (hg + 2) % G, c // G, [c % G])
                        if c == G and more1:
                            transpose_qk(s + 1)
                        if c < NS:
                            scores(s, hg, c)
                    transpose_max(s, hg)
                    if not (first and hg == 0):
                        attend(s - 1, (hg - 1) % G, range(4, 8), 8, False, False)
                        attend(s - 1, (hg - 1) % G, range(8, 10), 10, False, True)
                    for k in range(5):
                        t_scores(s, hg, 2 * k, more1)
                        t_scores(s, hg, 2 * k + 1, more1)
                        if k == 2:
                            attend(s, hg, range(0, 4), 4, True, False)
                        if k < 4:
                            slot_work(b, hg, k, first, last)

            pe.wait_ge(s_ident, 1)
            for t in range(TT):
                transpose_h(0, t)
            pe.wait_ge(s_wlo, G)
            pe.wait_ge(s_hT_lo, TT)
            for t in range(TT):
                project(0, 0, t)
            pe.wait_ge(s_raw, TT)
            pe.wait_ge(s_wlo, 2 * G)
            for t in range(TT):
                project(1, 1, t)
            transpose_qk(0)
            pe.wait_ge(s_const_v, 1)
            pe.wait_ge(s_const, 1)
            batches(pe, body)
            last = G * B - 1
            attend(last, 3, range(4, 8), 8, False, False)
            attend(last, 3, range(8, 10), 10, False, True)
            for t in range(TT):
                out_proj(B - 1, t, last)
            pe.wait_ge(s_x1, TT * B)
            for t in range(TT):
                transpose_q8(B - 1, t, last if t == 0 else None)
                ffn(B - 1, t)

        @block.scalar
        def _(act):
            x_t = x.rearrange("b (t p) d -> b p t d", p=P)

            def h_hi(b, t):
                act.wait_ge(s_hT, TT * b + t + 1)
                if t == 0 and not (isinstance(b, int) and b == 0):
                    act.wait_ge(s_qkv, TT * G * b)
                act.copy(hT_hi[:, t, :, :].rearrange("p g n -> p (g n)"), slot[t][:]).then_inc(s_hT_hi, 1)

            def copy_qkv(s, hg, t):
                act.wait_ge(s_qkv, TT * s + t + 1)
                if t == 0 and not (isinstance(s, int) and s == 0):
                    act.wait_ge(s_rsum, s)
                if t == 0 and not (isinstance(s, int) and s < 4):
                    act.wait_ge(s_pv, 3 * (s - 3))
                act.copy(qk[:, t, :], gp[t % 2][:, 0:2 * P]).then_inc(s_qk, 1)
                act.copy(v[:, hg, t, :], gp[t % 2][:, 2 * P:3 * P]).then_inc(s_raw, 1)

            def square(s):
                act.wait_ge(s_qk, TT * (s + 1))
                if isinstance(s, int) and s == 0:
                    act.wait_ge(s_fold, 6)
                act.activation(tmp[:], qk[:], ACT.Square).then_inc(s_sq, 1)

            def qk_hi(s):
                for i in range(2):
                    act.wait_ge(s_qkT, 2 * s + i + 1)
                    if i == 0 and not (isinstance(s, int) and s == 0):
                        act.wait_ge(s_bounce[0], 16 * s)
                    act.copy(qkT_hi[:, i, :], tp[i][:]).then_inc(s_qk_hi, 1)

            def exp(s, v):
                act.wait_ge(s_T, NST * s + v + 1)
                if not (isinstance(s, int) and s == 0) and v in (0, 4, 8):
                    act.wait_ge(s_pv, 3 * (s - 1) + v // 4 + 1)
                act.activation(prob[:, v, :], tp[v % 2][:], ACT.Exp, scale=SM_SCALE).then_inc(s_exp, 1)

            def att_hi(s, hg):
                act.wait_ge(s_att, s + 1)
                act.copy(attT_hi[:, hg, :], att[:]).then_inc(s_att_hi, 1)

            def q8_copy(p, t):
                n = TT * p + t
                act.wait_ge(s_qT, 2 + n + 1)
                act.copy(q8T[:].rearrange("p g n -> p (g n)"), slot[t % 2][:].bitcast(BF16)[:, 0:D]).then_inc(s_qTc, 1)

            def slot_work(b, hg, k, first, last):
                if hg == 1 and not last:
                    for t in ((), (0,), (1,), (2, 3))[k]:
                        h_hi(b + 1, t)
                if hg == 0 and first:
                    act.wait_ge(s_wq_T, k + 1)
                    act.copy(wffn_hi[:, :, k * P:(k + 1) * P],
                             slot[k][:].rearrange("p (g n) -> p g n", g=G)).then_inc(s_wffn_hi, 1)
                if hg >= 2 and not first and k % 2 == 0:
                    q8_copy(b - 1, 2 * (hg - 2) + k // 2)

            def body(b, first, last):
                for hg in range(G):
                    s = 4 * b + hg
                    more2 = not (last and hg >= 2)
                    if hg == 0 and not last:
                        act.wait_ge(s_hT, TT * (b + 1))
                        act.dma_start(xh[:], x_t[bass.ds(b + 1, 1)].rearrange("o p t d -> p (o t) d")).then_inc(s_x, 16)
                    if more2:
                        copy_qkv(s + 2, (hg + 2) % G, 0)
                    if not (last and hg == 3):
                        qk_hi(s + 1)
                    if more2:
                        for t in range(1, TT):
                            copy_qkv(s + 2, (hg + 2) % G, t)
                    act.wait_ge(s_mT, s + 1)
                    if not (first and hg == 0):
                        act.wait_ge(s_m, 16 * s)
                    act.mul(negmax[:], sp_[0][0:HG * TT, 0:P], -1.0).then_inc(s_mneg, 1)
                    if more2:
                        square(s + 2)
                    for k in range(5):
                        exp(s, 2 * k)
                        exp(s, 2 * k + 1)
                        if k < 4:
                            slot_work(b, hg, k, first, last)
                    if first and hg == 1:
                        act.wait_ge(s_wout_ld, 16)
                        act.copy(wout_hi[:], x1[:]).then_inc(s_wout_hi, 1)
                    if not (first and hg == 0):
                        if hg == 1 and not first:
                            act.wait_ge(s_op, TT * b)
                        att_hi(s - 1, (hg - 1) % G)

            def split_hi(lo, hi, i):
                act.copy(of_groups(wqkv_hi[:, i, :], lo, hi), of_groups(wq_stage[i], lo, hi)).then_inc(s_whi, 1)

            for i in range(G):
                act.wait_ge(s_wload[i], 16)
                split_hi(*W_PARTS[0], i)
                h_hi(0, i)
            for i in range(G):
                split_hi(*W_PARTS[1], i)
            for t in range(TT):
                copy_qkv(0, 0, t)
            square(0)
            for i in range(G):
                split_hi(*W_PARTS[2], i)
            for t in range(TT):
                copy_qkv(1, 1, t)
            qk_hi(0)
            square(1)
            act.wait_ge(s_wlo, G * len(W_PARTS))
            batches(act, body)
            att_hi(G * B - 1, 3)
            for t in range(TT):
                q8_copy(B - 1, t)

        @block.vector
        def _(dve):
            def ln_stats(b):
                dve.wait_ge(s_x, 16 * (b + 1))
                for t in range(TT):
                    dve.bn_stats(ln_st[:, t, :], xh[:, t, :]).then_inc(s_st, 1)
                dve.wait_ge(s_st, TT * (b + 1))
                dve.tensor_copy(wait_v[:], ones[:, 0:1])
                for t in range(TT):
                    dve.bn_aggr(ln_mv[:, t, :], ln_st[:, t, :]).then_inc(s_mv, 1)
                dve.wait_ge(s_mv, TT * (b + 1))
                dve.tensor_scalar(ln_var[:], ln_mv[:, :, 1], LN_EPS, None, ALU.add).then_inc(s_var, 1)

            def ln_apply(b):
                dve.wait_ge(s_rs, b + 1)
                for t in range(TT):
                    dve.tensor_scalar(xh[:, t, :], xh[:, t, :], ln_mv[:, t, 0:1], ln_rs[:, t:t + 1],
                                      ALU.subtract, ALU.mult).then_inc(s_h, 1)

            def h_lo(b, tiles):
                for t in tiles:
                    dve.wait_ge(s_hT_hi, TT * b + t + 1)
                    dve.tensor_tensor(hT_lo[:, t, :, :].rearrange("p g n -> p (g n)"), slot[t][:],
                                      f(hT_hi[:, t, :, :]).rearrange("p g n -> p (g n)"),
                                      ALU.subtract).then_inc(s_hT_lo, 1)

            def square_sums(s):
                dve.wait_ge(s_sq, s + 1)
                dve.tensor_reduce(ss[:], tmp[:].rearrange("p t (h n) -> p (t h) n", n=HD), AX.X, ALU.add).then_inc(s_ss, 1)
                dve.wait_ge(s_ss, s + 1)
                dve.tensor_scalar(ssv[:], ss[:], 1.0 / HD, RMS_EPS, ALU.mult, ALU.add).then_inc(s_ssv, 1)

            def rotate(s):
                raw = qk[:].rearrange("p t (i j n) -> p t i j n", i=2, j=HG)
                t4 = tmp[:].rearrange("p t (i j n) -> p t i j n", i=2, j=HG)
                for i in range(2):
                    for h in range(2):
                        src = raw[:, :, i, :, (1 - h) * HALF:(2 - h) * HALF]
                        sin = rope_s[:, i, :, h * HALF:(h + 1) * HALF].unsqueeze(2).to_broadcast([P, TT, HG, HALF])
                        dve.tensor_tensor(t4[:, :, i, :, h * HALF:(h + 1) * HALF], src, sin, ALU.mult).then_inc(s_sin, 1)

            def rotated(s):
                dve.wait_ge(s_sin, 4 * (s + 1))
                dve.wait_ge(s_cos, 2 * (s + 1))
                dve.tensor_tensor(rot[:], rot[:], tmp[:], ALU.add).then_inc(s_rsum, 1)

            def qk_lo(s):
                for i in range(2):
                    dve.wait_ge(s_qk_hi, 2 * s + i + 1)
                    if i == 0 and not (isinstance(s, int) and s == 0):
                        dve.wait_ge(s_bounce[1], 16 * s)
                    dve.tensor_tensor(qkT_lo[:, i, :], tp[i][:], f(qkT_hi[:, i, :]), ALU.subtract).then_inc(s_qk_lo, 1)

            def row_max(s, hg, u):
                if u == 0 and not (isinstance(s, int) and s < 2):
                    dve.wait_ge(s_mT, s - 1)
                m = rowmax[:, hg % 2, :].rearrange("p (j t) -> p j t", t=TT)
                t, heads = S_UNITS[u]
                dve.wait_ge(s_S, NS * s + u + 1)
                w = (t + 1) * P
                src = sp_[(NS * hg + u) % 2][:, 0:w * len(heads)].rearrange("p (j n) -> p j n", n=w)
                dve.tensor_reduce(m[:, heads[0]:heads[-1] + 1, t], src, AX.X, ALU.max).then_inc(s_max, 1)

            def normalise(s, k):
                if k == 0:
                    dve.wait_ge(s_pv, 3 * (s + 1))
                    if not (isinstance(s, int) and s == 0):
                        dve.wait_ge(s_att_lo, s)
                    dve.transpose(att[:], dn[:]).then_inc(s_dt, 1)
                elif k == 1:
                    dve.wait_ge(s_dt, s + 1)
                    dve.reciprocal(den_r[:], att[:].rearrange("p (c n) -> p c n", n=HD)[:, :, 0]).then_inc(s_dr, 1)
                elif k == 2:
                    dve.wait_ge(s_dr, s + 1)
                    dve.transpose(att[:], den_r[:].unsqueeze(2).to_broadcast([P, N // HD, HD])).then_inc(s_db, 1)
                else:
                    dve.wait_ge(s_db, s + 1)
                    dve.tensor_tensor(att[:], pv[:], att[:], ALU.mult).then_inc(s_att, 1)

            def quantise(k, src, scale, done, at):
                blk = src.rearrange("p (g n) -> p g n", g=G)
                if k > 0:
                    dve.wait_ge(done, at + k)
                if k == 0:
                    i = dve.tensor_reduce(amax[:], blk, AX.X, ALU.max, apply_absolute_value=True)
                elif k == 1:
                    i = dve.tensor_scalar(scale, amax[:], 1.0 / FP8_MAX, None, ALU.mult)
                elif k == 2:
                    i = dve.reciprocal(rscl[:], scale)
                elif k == 3:
                    i = dve.tensor_tensor(y[:].rearrange("p (g n) -> p g n", g=G), blk,
                                          rscl[:].unsqueeze(2).to_broadcast([P, G, P]), ALU.mult)
                elif k == 4:
                    i = dve.tensor_scalar(mag[:].bitcast(I32), y[:].bitcast(I32), EXPONENT_BITS, None, ALU.bitwise_and)
                else:
                    i = dve.tensor_scalar(mag[:], mag[:], FP8_MIN_NORMAL, ROUND_4BIT, ALU.max, ALU.mult)
                i.then_inc(done, 1)

            def ffn_moments(p):
                dve.wait_ge(s_fst, 9 * p + TT)
                dve.tensor_copy(wait_v[:], ones[:, 0:1])
                for t in range(TT):
                    dve.bn_aggr(f_mv[:, t, :], f_st[:, t, :]).then_inc(s_fst, 1)
                dve.wait_ge(s_fst, 9 * p + 2 * TT)
                dve.tensor_scalar(f_var[:], f_mv[:, :, 1], LN_EPS, None, ALU.add).then_inc(s_fst, 1)

            def ffn_quant(p, t, k):
                n = TT * p + t
                if k == 0:
                    dve.wait_ge(s_frs, p + 1)
                    if t > 0:
                        dve.wait_ge(s_q, QC * n)
                    dve.tensor_scalar(y[:], x1[:, t, :], f_mv[:, t, 0:1], f_rs[:, t:t + 1], ALU.subtract,
                                      ALU.mult).then_inc(s_h2, 1)
                else:
                    if k == 1:
                        dve.wait_ge(s_h2, n + 1)
                    quantise(k - 1, y[:], scl[:, t % 2, :], s_q, QC * n)

            def ffn_sum(p, t):
                n = TT * p + t
                for g in range(G):
                    dve.wait_ge(s_ff, G * n + g + 1)
                    if g:
                        dve.wait_ge(s_acc, summed(G * n + g))
                    a = x1[:, t, :]
                    dve.scalar_tensor_tensor(out=a, in0=slot[ffn_bank(t, g)][:], scalar=scl[:, t % 2, g:g + 1],
                                             in1=a, op0=ALU.mult, op1=ALU.add).then_inc(s_acc, 1)

            def out_sum(p, t):
                if t == 0:
                    dve.wait_ge(s_x1l, 16 * (p + 1))
                dve.wait_ge(s_op, TT * p + t + 1)
                dve.tensor_tensor(x1[:, t, :], slot[t][:], x1[:, t, :], ALU.add).then_inc(s_x1, 1)

            def ffn_stats(p, t):
                dve.wait_ge(s_x1, TT * p + t + 1)
                dve.bn_stats(f_st[:, t, :], x1[:, t, :]).then_inc(s_fst, 1)

            def wffn_quant(t):
                if t == 0:
                    dve.wait_ge(s_wffn_ld, 16 * TT)
                at = (QC + 1) * t
                for k in range(QC_V):
                    quantise(k, wffn_stage[t], scl[:, 0, :], s_wq, at)
                dve.wait_ge(s_wq, at + QC_V)
                dve.tensor_tensor(y[:], y[:], mag[:], ALU.add).then_inc(s_wq, 1)
                dve.wait_ge(s_wq, at + QC_V + 1)
                dve.tensor_tensor(y[:], y[:], mag[:], ALU.subtract).then_inc(s_wq, 1)
                dve.wait_ge(s_wq, at + QC)
                dve.tensor_tensor(wffn_stage[t].rearrange("p (g n) -> p g n", g=G), y[:].rearrange("p (g n) -> p g n", g=G),
                                  scl[:, 0, :].unsqueeze(2).to_broadcast([P, G, P]), ALU.mult).then_inc(s_wq, 1)
                dve.wait_ge(s_wq, at + QC + 1)

            def wffn_split(t):
                dve.wait_ge(s_wffn_hi, t + 1)
                cols = slice(t * P, (t + 1) * P)
                dve.tensor_tensor(wffn_lo[:, :, cols], slot[t][:].rearrange("p (g n) -> p g n", g=G),
                                  f(wffn_hi[:, :, cols]), ALU.subtract).then_inc(s_wffn_lo, 1)

            def body(b, first, last):
                for hg in range(G):
                    s = 4 * b + hg
                    more2 = not (last and hg >= 2)
                    quant = [2 * (hg - 2), 2 * (hg - 2) + 1] if hg >= 2 and not first else []
                    for u in range(NS):
                        row_max(s, hg, u)
                        if u == 5 and not (last and hg == 3):
                            qk_lo(s + 1)
                        if quant and 1 <= u <= QC_V + 1:
                            ffn_quant(b - 1, quant[0], u - 1)
                    if hg == 0 and not last:
                        ln_stats(b + 1)
                    if quant:
                        for k in range(5):
                            ffn_quant(b - 1, quant[1], k)
                    for k in range(4):
                        if not (first and hg == 0):
                            normalise(s - 1, k)
                        if quant and k < 2:
                            ffn_quant(b - 1, quant[1], k + 5)
                        if k == 2 and more2:
                            square_sums(s + 2)
                    if more2:
                        rotate(s + 2)
                    if quant:
                        ffn_sum(b - 1, quant[0])
                    if more2:
                        rotated(s + 2)
                    if hg == 0 and not last:
                        ln_apply(b + 1)
                    if first and hg == 0:
                        for t in range(2, TT):
                            wffn_quant(t)
                        for t in range(TT):
                            wffn_split(t)
                    if first and hg == 2:
                        dve.wait_ge(s_wout_hi, 1)
                        dve.tensor_tensor(wout_lo[:], x1[:], f(wout_hi[:]), ALU.subtract).then_inc(s_wout_lo, 1)
                    if hg == 1:
                        for k in range(4):
                            if not first:
                                for t in ((0, 1), (2,), (3,), ())[k]:
                                    out_sum(b - 1, t)
                            if not last:
                                h_lo(b + 1, ((), (0,), (1,), (2, 3))[k])
                        if not first:
                            for t in range(TT):
                                ffn_stats(b - 1, t)
                            ffn_moments(b - 1)
                    if quant:
                        ffn_sum(b - 1, quant[1])

            dve.memset(ones[:], 1.0).then_inc(s_const_v, 1)
            dve.wait_ge(s_const_v, 1)
            dve.memset(wait_v[:], 0.0).then_inc(s_acc, 1)
            for i in range(2):
                dve.memset(q8[:, i, 0:2], 0.0).then_inc(s_qT, 1)
            ln_stats(0)
            ln_apply(0)
            h_lo(0, range(TT))
            def split_lo(part):
                lo, hi = W_PARTS[part]
                for i in range(G):
                    dve.wait_ge(s_whi, G * part + i + 1)
                    dve.tensor_tensor(of_groups(wqkv_lo[:, i, :], lo, hi), of_groups(wq_stage[i], lo, hi),
                                      f(of_groups(wqkv_hi[:, i, :], lo, hi)), ALU.subtract).then_inc(s_wlo, 1)

            split_lo(0)
            split_lo(1)
            dve.wait_ge(s_tload, 48)
            for i in range(2):
                dve.tensor_tensor(rope_c[:, i], table[:, 0], gamma[:, i, :].unsqueeze(1).to_broadcast([P, TT, HD]),
                                  ALU.mult).then_inc(s_fold, 1)
                for h in range(2):
                    dve.tensor_tensor(rope_s[:, i, :, h * HALF:(h + 1) * HALF], table[:, 1, :, h * HALF:(h + 1) * HALF],
                                      gamma[:, i, (1 - h) * HALF:(2 - h) * HALF].unsqueeze(1).to_broadcast([P, TT, HALF]),
                                      ALU.mult).then_inc(s_fold, 1)
            dve.wait_ge(s_fold, 6)
            square_sums(0)
            rotate(0)
            rotated(0)
            split_lo(2)
            wffn_quant(0)
            qk_lo(0)
            square_sums(1)
            rotate(1)
            rotated(1)
            wffn_quant(1)
            batches(dve, body)
            for k in range(4):
                normalise(G * B - 1, k)
            p = B - 1
            for t in range(TT):
                out_sum(p, t)
                ffn_stats(p, t)
            ffn_moments(p)
            for t in range(TT):
                for k in range(QC_V + 1):
                    ffn_quant(p, t, k)
                if t > 0:
                    ffn_sum(p, t - 1)
            ffn_sum(p, TT - 1)

        @block.gpsimd
        def _(pool):
            def power(dst, src, done):
                pool.tensor_tensor(dst, src, half_neg[:, 0:src.shape[-1]], ALU.pow).then_inc(done, 1)

            def cos_part(s):
                raw = qk[:].rearrange("p t (i j n) -> p t i j n", i=2, j=HG)
                r = rot[:].rearrange("p t (i j n) -> p t i j n", i=2, j=HG)
                pool.wait_ge(s_qk, TT * (s + 1))
                if not (isinstance(s, int) and s == 0):
                    pool.wait_ge(s_qkT, 2 * s)
                for i in range(2):
                    cos = rope_c[:, i, :, :].unsqueeze(2).to_broadcast([P, TT, HG, HD])
                    pool.tensor_tensor(r[:, :, i], raw[:, :, i], cos, ALU.mult).then_inc(s_cos, 1)

            def head_norm(s):
                pool.wait_ge(s_ssv, s + 1)
                if not (isinstance(s, int) and s == 0):
                    pool.wait_ge(s_rope, s)
                power(rs[:], ssv[:], s_rrs)
                pool.wait_ge(s_rsum, s + 1)
                pool.wait_ge(s_rrs, s + 1)
                r = rot[:].rearrange("p t (h n) -> p (t h) n", n=HD)
                pool.tensor_tensor(r, r, rs[:].unsqueeze(2).to_broadcast([P, 2 * HG * TT, HD]), ALU.mult).then_inc(s_rope, 1)

            def round_fp8(n, t):
                at = QC * n + QC_V
                pool.wait_ge(s_q, at)
                pool.tensor_tensor(y[:], y[:], mag[:], ALU.add).then_inc(s_q, 1)
                pool.wait_ge(s_q, at + 1)
                pool.wait_ge(s_qT, n + 1)
                pool.tensor_tensor(q8[:, t % 2, :], y[:], mag[:], ALU.subtract).then_inc(s_q, 1)

            def att_lo(s, hg):
                pool.wait_ge(s_att_hi, s + 1)
                pool.tensor_tensor(attT_lo[:, hg, :], att[:], f(attT_hi[:, hg, :]), ALU.subtract).then_inc(s_att_lo, 1)

            def ln_power(b):
                pool.wait_ge(s_var, b + 1)
                power(ln_rs[:], ln_var[:], s_rs)

            def ffn_power(p):
                pool.wait_ge(s_fst, 9 * (p + 1))
                power(f_rs[:], f_var[:], s_frs)

            def body(b, first, last):
                for hg in range(G):
                    s = 4 * b + hg
                    if hg == 0 and not last:
                        ln_power(b + 1)
                    if hg == 2 and not first:
                        ffn_power(b - 1)
                    t = 2 * (hg - 2)
                    if hg >= 2 and not first:
                        round_fp8(TT * (b - 1) + t, t)
                    if not (last and hg >= 2):
                        cos_part(s + 2)
                    if hg >= 2 and not first:
                        round_fp8(TT * (b - 1) + t + 1, t + 1)
                    if not (last and hg >= 2):
                        head_norm(s + 2)
                    if not (first and hg == 0):
                        att_lo(s - 1, (hg - 1) % G)

            def step(ins, count=[0]):
                count[0] += 1
                ins.then_inc(s_pool_c, 1)
                pool.wait_ge(s_pool_c, count[0])

            step(pool.memset(half_neg[:], -0.5))
            step(pool.memset(ident[:], 0.0))
            pool.affine_select(ident[:], ident[:], pattern=[[-1, P]], compare_op=ALU.not_equal, fill=1.0,
                               base=0, channel_multiplier=1).then_inc(s_ident, 1)
            ln_power(0)
            pool.wait_ge(s_ident, 1)
            step(pool.tensor_copy(ident_bf[:], ident[:]))
            step(pool.memset(mask_q[:], 0.0))
            step(pool.affine_select(mask_q[:], mask_q[:], pattern=[[-1, P]], compare_op=ALU.is_ge, fill=NEG,
                                    base=0, channel_multiplier=1))
            step(pool.memset(mask_k[:], 0.0))
            step(pool.memset(f(k_stack[SHIFT_ROW:SHIFT_ROW + HD, :, :, :]), 1.0))
            pool.affine_select(mask_k[:], mask_k[:], pattern=[[1, P]], compare_op=ALU.is_ge, fill=NEG,
                               base=0, channel_multiplier=-1).then_inc(s_const, 1)
            pool.wait_ge(s_fold, 6)
            for g in range(2):
                cos_part(g)
                head_norm(g)
            batches(pool, body)
            att_lo(G * B - 1, 3)
            ffn_power(B - 1)
            for t in range(TT):
                round_fp8(TT * (B - 1) + t, t)


_NAMES = ["L0_attn_x", "L0_attn_w_qkv", "L0_attn_w_out", "L0_attn_q_gamma", "L0_attn_k_gamma", "L0_ffn_weight"]


def kernel(**inputs):
    import numpy as _np
    import concourse.bacc as _bacc
    from concourse import mybir as _mybir
    from concourse.bass_utils import run_bass_kernel_spmd as _run

    nc = _bacc.Bacc("TRN2", target_bir_lowering=False, num_devices=1, dynamic_dma_scratch_size=512)
    arrays = {f"in_{n}": _np.ascontiguousarray(inputs[n]) for n in _NAMES}
    arrays["in_rope"] = rope_tables()
    args = [nc.dram_tensor(n, a.shape, _mybir.dt.from_np(a.dtype), kind="ExternalInput").ap() for n, a in arrays.items()]
    args.append(nc.dram_tensor("out_0", (B, N, D), _mybir.dt.float32, kind="ExternalOutput").ap())
    build_program(nc, *args)
    r = _run(nc, [arrays], core_ids=[0])
    return r.results[0]["out_0"]
```

```python
from contextlib import ExitStack

import numpy as np

import concourse.bass as bass
from concourse import mybir

ALU = mybir.AluOpType
ACT = mybir.ActivationFunctionType
AX = mybir.AxisListType
F32 = mybir.dt.float32
F32R = mybir.dt.float32r
BF16 = mybir.dt.bfloat16
I32 = mybir.dt.int32

P = 128
B, N, D = 4, 512, 512
HD = 32
HALF = HD // 2
HG = P // HD
G = D // P
TT = N // P
QKV_G = 3 * P
SPLIT_ROWS = 3 * HD
SHIFT_ROW = SPLIT_ROWS
LN_EPS = 1e-5
RMS_EPS = 1e-6
THETA = 10000.0
NEG = -1e30
FP8_MAX = 448.0
FP8_MIN_NORMAL = 2.0 ** -6
ROUND_4BIT = 1.5 * 2.0 ** 20
EXPONENT_BITS = 0x7F800000
SM_SCALE = 1.0 / float(np.sqrt(HD))

S_UNITS = ([(0, (0, 1, 2, 3))] + [(1, (0, 1)), (1, (2, 3))]
           + [(2, (j,)) for j in range(HG)] + [(3, (j,)) for j in range(HG)])
NS = len(S_UNITS)
ST_UNITS = ([[(j, 0, 0)] for j in range(HG)]
            + [[(j, 1, 0), (j, 3, N - P)] for j in range(HG)]
            + [[(j, 2, 0), (j + 1, 2, N // 2)] for j in (0, 2)])
NST = len(ST_UNITS)
STACKS = 6
QC = 8
QC_V = 6
OUT_AT = {(0, 4): (0, 1), (1, 0): (2,), (1, 1): (3,)}
H_AT = ((), (), (0, 1), (2, 3), ())
Q8_AT = (0, 2)
FFN_AT = (1, 3)
SCORES_AT = (0, 1, 2, 4, 5, 6, 7, 9, 10, 11, 12)
MAX_AT = 14
def ffn_bank(t, g):
    return (t % 2 + 1 + g) % 4


def rope_tables():
    inv = (np.float32(1.0) / np.power(np.float32(THETA), np.arange(0, HD, 2, dtype=np.float32) / np.float32(HD),
                                      dtype=np.float32)).astype(np.float32)
    freqs = (np.arange(N, dtype=np.float32)[:, None] * inv[None, :]).astype(np.float32)
    cos, sin = np.cos(freqs.astype(np.float64)), np.sin(freqs.astype(np.float64))
    both = np.stack([np.concatenate([cos, cos], 1), np.concatenate([-sin, sin], 1)], 0).astype(np.float32)
    return np.ascontiguousarray(both.reshape(2, TT, P, HD).transpose(2, 0, 1, 3))


def build_program(nc, x, w_qkv, w_out, q_gamma, k_gamma, w_ffn, rope, out):
    with ExitStack() as ctx:
        def sb(name, shape, dt=F32):
            return ctx.enter_context(nc.sbuf_tensor(name, shape, dt))

        def ps(name, shape, dt=F32):
            return ctx.enter_context(nc.psum_tensor(name, shape, dt))

        def sem(name):
            return ctx.enter_context(nc.semaphore(name))

        wqkv_hi = sb("wqkv_hi", [P, G, 3 * D], F32R)
        wqkv_lo = sb("wqkv_lo", [P, G, 3 * D], F32R)
        wout_hi = sb("wout_hi", [P, G, D], F32R)
        wout_lo = sb("wout_lo", [P, G, D], F32R)
        wffn_hi = sb("wffn_hi", [P, G, D], F32R)
        wffn_lo = sb("wffn_lo", [P, G, D], F32R)
        ident = sb("ident", [P, P])
        ident_bf = sb("ident_bf", [P, P], BF16)
        mask_q = sb("mask_q", [P, P], BF16)
        mask_k = sb("mask_k", [P, P], BF16)
        ones = sb("ones", [P, HD])
        wait_v = sb("wait_v", [P, 1])
        half_neg = sb("half_neg", [P, 2 * HG * TT])
        rope_c = sb("rope_c", [P, 2, TT, HD])
        rope_s = sb("rope_s", [P, 2, TT, HD])
        xh = sb("xh", [P, TT, D])
        ln_st = sb("ln_st", [P, TT, 6])
        ln_mv = sb("ln_mv", [P, TT, 2])
        ln_var = sb("ln_var", [P, TT])
        ln_rs = sb("ln_rs", [P, TT])
        ln_nm = sb("ln_nm", [P, TT])
        hT_hi = sb("hT_hi", [P, TT, G, P], F32R)
        hT_lo = sb("hT_lo", [P, TT, G, P], F32R)
        qk = sb("qk", [P, TT, 2 * P])
        v = sb("v", [P, G, TT, P])
        rot = sb("rot", [P, TT, 2 * P])
        tmp = sb("tmp", [P, TT, 2 * P])
        ss = sb("ss", [P, 2 * HG * TT])
        ssv = sb("ssv", [P, 2 * HG * TT])
        rs = sb("rs", [P, 2 * HG * TT])
        table = tmp[:, 0, 0:2 * TT * HD].rearrange("p (c t n) -> p c t n", c=2, t=TT)
        gamma = tmp[:, 1, 0:2 * HD].rearrange("p (i n) -> p i n", i=2)
        qkT_hi = sb("qkT_hi", [P, 2, N], F32R)
        qkT_lo = sb("qkT_lo", [P, 2, N], F32R)
        q_stack = sb("q_stack", [P, 2, HG, N], F32R)
        k_stack = sb("k_stack", [P, 2, HG, N], F32R)
        bounce = nc.dram_tensor("bounce", (2, 2, 2, P, N), F32, kind="Internal").ap()
        rowmax = sb("rowmax", [P, 2, HG * TT])
        negmax = sb("negmax", [HG * TT, P], F32R)
        prob = sb("prob", [P, NST, N])
        den_r = sb("den_r", [P, N // HD])
        att = sb("att", [P, N])
        attT_hi = sb("attT_hi", [P, G, N], F32R)
        attT_lo = sb("attT_lo", [P, G, N], F32R)
        x1 = sb("x1", [P, TT, D])
        f_st = sb("f_st", [P, TT, 6])
        f_mv = sb("f_mv", [P, TT, 2])
        f_var = sb("f_var", [P, TT])
        f_rs = sb("f_rs", [P, TT])
        f_nm = sb("f_nm", [P, TT])
        amax = sb("amax", [P, G])
        scl = sb("scl", [P, TT, G])
        rscl = sb("rscl", [P, G])
        y = sb("y", [P, D])
        mag = sb("mag", [P, D])
        q8 = sb("q8", [P, 2, D], BF16)
        q8T = sb("q8T", [P, G, P], F32R)

        gp = [ps(f"gp{i}", [P, 512]) for i in range(2)]
        sp_ = [ps(f"sp{i}", [P, 512]) for i in range(2)]
        tp = [ps(f"tp{i}", [P, 512]) for i in range(2)]
        pv = ps("pv", [P, 512])
        dn = ps("dn", [P, 512])
        slot = gp + sp_

        s_wload = [sem(f"w_loaded{i}") for i in range(G)]
        s_wrest = sem("w_rest_loaded")
        s_tload = sem("tables_loaded")
        s_const = sem("constants_ready")
        s_ident = sem("identity_ready")
        s_pool_c = sem("constants_step")
        s_const_v = sem("vector_constants_ready")
        s_fold = sem("tables_folded")
        s_whi = sem("wqkv_hi_ready")
        s_wlo = sem("wqkv_lo_ready")
        s_wout_ld = sem("wout_loaded")
        s_wout_hi = sem("wout_hi_ready")
        s_wout_lo = sem("wout_lo_ready")
        s_wffn_ld = sem("wffn_loaded")
        s_wq = sem("wffn_quant_step")
        s_wq_T = sem("wffn_transposed")
        s_wffn_hi = sem("wffn_hi_ready")
        s_wffn_lo = sem("wffn_lo_ready")
        s_x = sem("x_loaded")
        s_st = sem("ln_stats")
        s_mv = sem("ln_moments")
        s_var = sem("ln_var_eps")
        s_rs = sem("ln_rstd")
        s_nm = sem("ln_shift")
        s_h = sem("h_ready")
        s_hT = sem("h_transposed")
        s_hT_hi = sem("hT_hi_ready")
        s_hT_lo = sem("hT_lo_ready")
        s_qkv = sem("qkv_done")
        s_raw = sem("qkv_copied")
        s_qk = sem("qk_copied")
        s_sq = sem("squares_ready")
        s_ss = sem("square_sums")
        s_ssv = sem("mean_squares")
        s_rrs = sem("head_rstd")
        s_cos = sem("cos_part")
        s_sin = sem("sin_part")
        s_rsum = sem("rotated")
        s_rope = sem("qk_ready")
        s_qkT = sem("qk_transposed")
        s_qk_hi = sem("qkT_hi_ready")
        s_qk_lo = sem("qkT_lo_ready")
        s_stack = sem("stack_loaded")
        s_S = sem("scores_done")
        s_max = sem("rowmax_ready")
        s_mT = sem("rowmax_transposed")
        s_mneg = sem("negmax_ready")
        s_m = sem("shift_loaded")
        s_T = sem("t_scores_done")
        s_exp = sem("exp_done")
        s_pv = sem("pv_done")
        s_dt = sem("den_transposed")
        s_dr = sem("den_reciprocal")
        s_db = sem("den_broadcast")
        s_att = sem("att_ready")
        s_att_hi = sem("attT_hi_ready")
        s_att_lo = sem("attT_lo_ready")
        s_x1l = sem("residual_loaded")
        s_op = sem("out_proj_done")
        s_x1 = sem("x1_ready")
        s_fst = sem("ffn_ln_step")
        s_h2 = sem("ffn_h_ready")
        s_frs = sem("ffn_rstd")
        s_fnm = sem("ffn_ln_shift")
        s_q = [sem(f"quant_step{t}") for t in range(TT)]
        s_qT = sem("q8_transposed")
        s_qTc = sem("q8T_ready")
        s_ff = sem("ffn_done")
        s_acc = sem("acc_step")
        s_out = sem("out_stored")
        s_bounce = [sem(f"bounce_written{i}") for i in range(2)]

        wq_stage = [prob[:, 3 * i:3 * i + 3, :].rearrange("p a n -> p (a n)") for i in range(3)]
        wq_stage.append(x1[:, 0:3, :].rearrange("p a n -> p (a n)"))
        wffn_stage = [x1[:, 3, :], prob[:, 9, :], att[:], v[:, 3].rearrange("p t n -> p (t n)")]

        def of_groups(w, lo, hi):
            return w.rearrange("p (c n) -> p c n", c=3)[:, :, lo * P:hi * P]

        W_PARTS = ((0, 1), (1, 2), (2, G))

        def f(ap):
            return ap.bitcast(F32)

        def quant_bufs(t, tail=False):
            if tail and t >= 2:
                return prob[:, 2 * t, :], prob[:, 2 * t + 1, :]
            return (xh[:, 2, :], xh[:, 3, :]) if t % 2 else (y[:], mag[:])

        def summed(n):
            return n + 1

        def batches(eng, body):
            body(0, True, False)
            with eng.Fori(1, B - 1) as b:
                body(b, False, False)
            body(B - 1, False, True)

        def sin_part(eng, s):
            raw = qk[:].rearrange("p t (i j n) -> p t i j n", i=2, j=HG)
            t4 = tmp[:].rearrange("p t (i j n) -> p t i j n", i=2, j=HG)
            eng.wait_ge(s_ss, s + 1)
            for i in range(2):
                for h in range(2):
                    src = raw[:, :, i, :, (1 - h) * HALF:(2 - h) * HALF]
                    sin = rope_s[:, i, :, h * HALF:(h + 1) * HALF].unsqueeze(2).to_broadcast([P, TT, HG, HALF])
                    eng.tensor_tensor(t4[:, :, i, :, h * HALF:(h + 1) * HALF], src, sin, ALU.mult).then_inc(s_sin, 1)

        block = ctx.enter_context(nc.Block())

        @block.sync
        def _(q):
            x_t = x.rearrange("b (t p) d -> b p t d", p=P)
            out_t = out.rearrange("b (t p) d -> b t p d", p=P)

            def stack(s, hg):
                for i, (src, ready) in enumerate(((qkT_hi, s_qk_hi), (qkT_lo, s_qk_lo))):
                    q.wait_ge(ready, 2 * (s + 1))
                    q.dma_start(bounce[hg % 2, i].rearrange("c p n -> p c n"), f(src[:])).then_inc(s_bounce[i], 16)
                for r, i in ((0, 0), (1, 0), (2, 0), (2, 1), (1, 1), (0, 1)):
                    part = int((r, i) in ((2, 0), (1, 1)))
                    q.wait_ge(s_bounce[part], 16 * (s + 1))
                    q.dma_start(f((q_stack, k_stack)[i][r * HD:(r + 1) * HD, hg % 2, :, :]),
                                bounce[hg % 2, part, i].rearrange("(j p) n -> p j n", p=HD)).then_inc(s_stack, 16)

            def store(p, tiles):
                for t in tiles:
                    q.wait_ge(s_acc, summed(G * (4 * p + t + 1)))
                    q.dma_start(out_t[bass.ds(p, 1), t].rearrange("o p d -> p (o d)"),
                                x1[:, t, :]).then_inc(s_out, 16)

            q.dma_start(xh[:], x_t[0]).then_inc(s_x, 16)
            for lo, hi, done in ((0, 1, s_wload), (1, G, [s_wrest] * G)):
                for i in range(G):
                    q.dma_start(of_groups(wq_stage[i], lo, hi), of_groups(w_qkv[i * P:(i + 1) * P, :], lo, hi)).then_inc(done[i], 16)
            q.dma_start(table, rope).then_inc(s_tload, 16)
            q.dma_start(gamma[:, 0, :], q_gamma.rearrange("(o n) -> o n", o=1).to_broadcast([P, HD])).then_inc(s_tload, 16)
            q.dma_start(gamma[:, 1, :], k_gamma.rearrange("(o n) -> o n", o=1).to_broadcast([P, HD])).then_inc(s_tload, 16)
            for t in range(TT):
                q.dma_start(wffn_stage[t], w_ffn[t * P:(t + 1) * P, :]).then_inc(s_wffn_ld, 16)
            stack(0, 0)

            def body(b, first, last):
                for hg in range(G):
                    s = 4 * b + hg
                    if not (last and hg == 3):
                        stack(s + 1, (hg + 1) % G)
                    if first and hg == 0:
                        q.wait_ge(s_wq_T, G)
                        q.dma_start(x1[:], w_out.rearrange("(g p) n -> p g n", p=P)).then_inc(s_wout_ld, 16)
                    if first and hg == 3:
                        q.wait_ge(s_wout_lo, 1)
                    if hg == 3:
                        if not first:
                            store(b - 1, range(TT))
                            q.wait_ge(s_out, 16 * TT * b)
                        q.dma_start(x1[:], x_t[bass.ds(b, 1)].rearrange("o p t d -> p (o t) d")).then_inc(s_x1l, 16)

            batches(q, body)
            store(B - 1, range(TT))
            q.wait_ge(s_out, 16 * B * TT)

        @block.tensor
        def _(pe):
            def split_product(dst, a_hi, a_lo, w_hi, w_lo, n):
                for i in range(n):
                    pe.matmul(dst, a_hi(i), w_hi(i), start=(i == 0), stop=False)
                    pe.matmul(dst, a_hi(i), w_lo(i), start=False, stop=False)
                    mm = pe.matmul(dst, a_lo(i), w_hi(i), start=False, stop=(i == n - 1))
                return mm

            def banks_free(s):
                pe.wait_ge(s_mneg, s + 1)
                pe.wait_ge(s_raw, min(TT * (s + 3), TT * G * B) if isinstance(s, int) else TT * (s + 3))

            def step_start(b, hg, first, last):
                s = 4 * b + hg
                if hg == 1 and first:
                    pe.wait_ge(s_wffn_lo, G)
                if first and hg == 0:
                    pe.wait_ge(s_wffn_lo, 2)
                    pe.wait_ge(s_wlo, G * len(W_PARTS))
                    return
                banks_free(s - 1)
                if hg == 0:
                    pe.wait_ge(s_acc, summed(G * TT * (b - 1)))
                if hg == 1 and not first:
                    pe.wait_ge(s_x1, TT * (b - 1) + 2)
                if hg == 2 and not last:
                    pe.wait_ge(s_hT_lo, TT * (b + 2))
                if hg == 2 and not first:
                    pe.wait_ge(s_x1, TT * b)
                if hg == 3 and not first:
                    pe.wait_ge(s_acc, summed(G * (TT * (b - 1) + 2)))

            def transpose_h(b, t):
                pe.wait_ge(s_h, TT * b + t + 1)
                if isinstance(b, int) and b == 0:
                    pass
                elif isinstance(b, int) and b == 1:
                    if t == 0:
                        banks_free(1)
                else:
                    pe.wait_ge(s_x1, TT * (b - 2) + t + 1)
                for g in range(G):
                    mm = pe.transpose(slot[t][:, g * P:(g + 1) * P], xh[:, t, g * P:(g + 1) * P], ident[:])
                mm.then_inc(s_hT, 1)

            def project(s, hg, t, blocks=range(G)):
                if blocks[0] == 0 and t >= 2:
                    pe.wait_ge(s_raw, TT * s + t - 1)
                a_hi, a_lo = hT_hi[:, t], hT_lo[:, t]
                dst = gp[t % 2][:, 0:QKV_G]
                w_hi, w_lo = (w.rearrange("p g (c n) -> p g c n", c=3)[:, :, :, hg * P:(hg + 1) * P]
                              for w in (wqkv_hi[:], wqkv_lo[:]))
                for i in blocks:
                    pe.matmul(dst, a_hi[:, i, :], w_hi[:, i], start=(i == 0), stop=False)
                    pe.matmul(dst, a_hi[:, i, :], w_lo[:, i], start=False, stop=False)
                    mm = pe.matmul(dst, a_lo[:, i, :], w_hi[:, i], start=False, stop=(i == G - 1))
                if blocks[-1] == G - 1:
                    mm.then_inc(s_qkv, 1)

            def transpose_qk(s):
                pe.wait_ge(s_rope, s + 1)
                if not (isinstance(s, int) and s < 2):
                    pe.wait_ge(s_exp, NST * (s - 1))
                for i in range(2):
                    for t in range(TT):
                        mm = pe.transpose(tp[i][:, t * P:(t + 1) * P], rot[:, t, i * P:(i + 1) * P], ident[:])
                    mm.then_inc(s_qkT, 1)

            def scores(s, hg, u):
                t, heads = S_UNITS[u]
                if u == 0:
                    pe.wait_ge(s_stack, 16 * STACKS * (s + 1))
                if not (isinstance(s, int) and s == 0 and u < 2):
                    pe.wait_ge(s_max, NS * s + u - 1)
                bank = sp_[(NS * hg + u) % 2]
                q_st, k_st = q_stack[0:SPLIT_ROWS, hg % 2], k_stack[0:SPLIT_ROWS, hg % 2]
                width = (t + 1) * P
                n = len(heads)
                pe.matmul(bank[:, 0:n * width].rearrange("p (j n) -> p j n", n=width)[:, :, t * P:width],
                          ident_bf[:], mask_q[:].unsqueeze(1).to_broadcast([P, n, P]), start=True, stop=False,
                          skip_group_check=True)
                for i, j in enumerate(heads):
                    lo = i * width
                    mm = pe.matmul(bank[:, lo:lo + width], q_st[:, j, t * P:(t + 1) * P],
                                   k_st[:, j, 0:width], start=False, stop=True,
                                   skip_group_check=True)
                mm.then_inc(s_S, 1)

            def transpose_max(s, hg):
                pe.wait_ge(s_max, NS * (s + 1))
                pe.transpose(sp_[0][0:HG * TT, 0:P], rowmax[:, hg % 2, :], ident[:]).then_inc(s_mT, 1)

            def t_scores(s, hg, v, more1):
                if v == 0:
                    pe.wait_ge(s_m, 16 * (s + 1))
                if v < 2 and more1:
                    pe.wait_ge(s_qk_lo, 2 * (s + 1) + v + 1)
                else:
                    pe.wait_ge(s_exp, NST * s + v - 1)
                bank = tp[v % 2]
                q_st, k_st = q_stack[0:SHIFT_ROW + 1, hg % 2], k_stack[0:SHIFT_ROW + 1, hg % 2]
                n, step = len(ST_UNITS[v]), max(1, ST_UNITS[v][-1][2] // P)
                pe.matmul(bank[:].rearrange("p (a n) -> p a n", n=P)[:, 0:(n - 1) * step + 1:step, :],
                          ident_bf[:], mask_k[:].unsqueeze(1).to_broadcast([P, n, P]), start=True, stop=False,
                          skip_group_check=True)
                for j, kt, lo in ST_UNITS[v]:
                    width = N - kt * P
                    mm = pe.matmul(bank[:, lo:lo + width], k_st[:, j, kt * P:(kt + 1) * P],
                                   q_st[:, j, kt * P:N], start=False, stop=True,
                                   skip_group_check=True)
                mm.then_inc(s_T, 1)

            def attend(s, hg, units, need, first_chunk, last_chunk, sums=(False, True)):
                pe.wait_ge(s_exp, NST * s + need)
                if first_chunk and not (isinstance(s, int) and s == 0):
                    pe.wait_ge(s_att, s)
                by_kt = {}
                for u in units:
                    for j, kt, lo in ST_UNITS[u]:
                        by_kt.setdefault(kt, []).append((u, j, lo))
                for sum_only in sums:
                    dst = dn if sum_only else pv
                    for n, (kt, parts) in enumerate(by_kt.items()):
                        for u, j, lo in parts:
                            c = slice(j * HD, (j + 1) * HD)
                            lhs = ones[:] if sum_only else v[:, hg, kt, j * HD:(j + 1) * HD]
                            mm = pe.matmul(dst[c, kt * P:N], lhs, prob[:, u, lo:lo + N - kt * P],
                                           start=(kt == 0), stop=(last_chunk and n == len(by_kt) - 1),
                                           skip_group_check=True)
                if True in sums:
                    mm.then_inc(s_pv, 1)

            def out_proj(p, t, s):
                if t == 0:
                    pe.wait_ge(s_att_lo, G * (p + 1))
                if t in (0, 2):
                    banks_free(s)
                cols = slice(t * P, (t + 1) * P)
                split_product(slot[t][:], lambda i: attT_hi[:, i, cols], lambda i: attT_lo[:, i, cols],
                              lambda i: wout_hi[:, i, :], lambda i: wout_lo[:, i, :], G).then_inc(s_op, 1)

            def transpose_q8(p, t, s):
                n = TT * p + t
                pe.wait_ge(s_q[t], QC * (p + 1))
                if t == 0 or (t == 2 and s is not None):
                    banks_free(s)
                elif t == 2:
                    pe.wait_ge(s_acc, summed(G * (n - 1) + 3))
                else:
                    pe.wait_ge(s_acc, summed(G * (n - 1) + 1))
                for g in range(G):
                    mm = pe.transpose(slot[t % 2][:].bitcast(BF16)[:, g * P:(g + 1) * P],
                                      q8[:, t % 2, g * P:(g + 1) * P], ident_bf[:])
                mm.then_inc(s_qT, 1)

            def ffn(p, t):
                n = TT * p + t
                pe.wait_ge(s_qTc, n + 1)
                for g in range(G):
                    if t % 2 == 1 and g <= 2:
                        pe.wait_ge(s_acc, summed(G * (n - 1) + g + 2))
                    if t == 2 and g == 0:
                        pe.wait_ge(s_acc, summed(G * n))
                    bank = slot[ffn_bank(t, g)]
                    pe.matmul(bank[:], q8T[:, g, :], wffn_hi[:, g, :], start=True, stop=False)
                    pe.matmul(bank[:], q8T[:, g, :], wffn_lo[:, g, :], start=False, stop=True).then_inc(s_ff, 1)

            def transpose_wffn(t):
                pe.wait_ge(s_wq, (QC + 1) * (t + 1))
                if t < 2:
                    pe.wait_ge(s_raw, TT * 2)
                for g in range(G):
                    mm = pe.transpose(slot[t][:, g * P:(g + 1) * P], wffn_stage[t][:, g * P:(g + 1) * P], ident[:])
                mm.then_inc(s_wq_T, 1)

            def slot_work(b, hg, k, first, last):
                s = 4 * b + hg
                if not first and (hg, k) in OUT_AT:
                    for t in OUT_AT[hg, k]:
                        out_proj(b - 1, t, s)
                if hg == 1 and not last:
                    for t in H_AT[k]:
                        transpose_h(b + 1, t)
                if first and hg == 0 and k in (2, 3):
                    banks_free(s)
                    transpose_wffn(k)
                if hg >= 2 and not first and k in Q8_AT:
                    transpose_q8(b - 1, 2 * (hg - 2) + Q8_AT.index(k), s)
                if hg >= 2 and not first and k in FFN_AT:
                    ffn(b - 1, 2 * (hg - 2) + FFN_AT.index(k))

            def body(b, first, last):
                for hg in range(G):
                    s = 4 * b + hg
                    more1 = not (last and hg == 3)
                    more2 = not (last and hg >= 2)
                    step_start(b, hg, first, last)
                    delay = G if first and hg == 0 else 0
                    for c in range(G * TT + delay):
                        if more2 and c < G * TT:
                            project(s + 2, (hg + 2) % G, c // G, [c % G])
                        if c == G + delay and more1:
                            transpose_qk(s + 1)
                        if c - delay in SCORES_AT:
                            scores(s, hg, SCORES_AT.index(c - delay))
                        if c == MAX_AT + delay:
                            transpose_max(s, hg)
                    if not (first and hg == 0):
                        attend(s - 1, (hg - 1) % G, range(4, 8), 8, False, False)
                        attend(s - 1, (hg - 1) % G, range(8, 10), 10, False, True)
                    for k in range(5):
                        slot_work(b, hg, k, first, last)
                        t_scores(s, hg, 2 * k, more1)
                        t_scores(s, hg, 2 * k + 1, more1)
                        if k == 2:
                            attend(s, hg, range(0, 4), 4, True, False, (False,))
                    attend(s, hg, range(0, 4), 4, False, False, (True,))

            pe.wait_ge(s_ident, 1)
            for t in range(TT):
                transpose_h(0, t)
            pe.wait_ge(s_wlo, G)
            pe.wait_ge(s_hT_lo, TT)
            for t in range(TT):
                project(0, 0, t)
            pe.wait_ge(s_raw, TT)
            pe.wait_ge(s_wlo, 2 * G)
            for t in range(TT):
                project(1, 1, t)
            transpose_qk(0)
            for t in range(2):
                transpose_wffn(t)
            pe.wait_ge(s_const_v, 1)
            pe.wait_ge(s_const, 1)
            batches(pe, body)
            last = G * B - 1
            attend(last, 3, range(4, 8), 8, False, False)
            attend(last, 3, range(8, 10), 10, False, True)
            banks_free(last)
            pe.wait_ge(s_acc, summed(G * TT * (B - 1)))
            for groups in (range(G - 1), range(G - 1, G)):
                pe.wait_ge(s_att_lo, G * (B - 1) + groups[-1] + 1)
                for t in range(TT):
                    cols = slice(t * P, (t + 1) * P)
                    for i in groups:
                        pe.matmul(slot[t][:], attT_hi[:, i, cols], wout_hi[:, i, :], start=(i == 0), stop=False)
                        pe.matmul(slot[t][:], attT_hi[:, i, cols], wout_lo[:, i, :], start=False, stop=False)
                        mm = pe.matmul(slot[t][:], attT_lo[:, i, cols], wout_hi[:, i, :], start=False, stop=(i == G - 1))
                    if groups[-1] == G - 1:
                        mm.then_inc(s_op, 1)
            for t in range(TT):
                if t < 2:
                    pe.wait_ge(s_x1, TT * B)
                transpose_q8(B - 1, t, last if t == 0 else None)
                ffn(B - 1, t)

        @block.scalar
        def _(act):
            x_t = x.rearrange("b (t p) d -> b p t d", p=P)

            def h_hi(b, t):
                act.wait_ge(s_hT, TT * b + t + 1)
                if t == 0 and not (isinstance(b, int) and b == 0):
                    act.wait_ge(s_qkv, TT * G * b)
                act.copy(hT_hi[:, t, :, :].rearrange("p g n -> p (g n)"), slot[t][:]).then_inc(s_hT_hi, 1)

            def copy_qkv(s, hg, t):
                act.wait_ge(s_qkv, TT * s + t + 1)
                if t == 0 and not (isinstance(s, int) and s == 0):
                    act.wait_ge(s_rsum, s)
                if t == 0 and not (isinstance(s, int) and s < 4):
                    act.wait_ge(s_pv, 3 * (s - 3))
                act.copy(qk[:, t, :], gp[t % 2][:, 0:2 * P]).then_inc(s_qk, 1)
                act.copy(v[:, hg, t, :], gp[t % 2][:, 2 * P:3 * P]).then_inc(s_raw, 1)

            def square(s):
                act.wait_ge(s_qk, TT * (s + 1))
                if isinstance(s, int) and s == 0:
                    act.wait_ge(s_fold, 6)
                act.activation(tmp[:], qk[:], ACT.Square).then_inc(s_sq, 1)

            def qk_hi(s):
                for i in range(2):
                    act.wait_ge(s_qkT, 2 * s + i + 1)
                    if i == 0 and not (isinstance(s, int) and s == 0):
                        act.wait_ge(s_bounce[0], 16 * s)
                    act.copy(qkT_hi[:, i, :], tp[i][:]).then_inc(s_qk_hi, 1)

            def exp(s, v):
                act.wait_ge(s_T, NST * s + v + 1)
                if not (isinstance(s, int) and s == 0) and v in (0, 4, 8):
                    act.wait_ge(s_pv, 3 * (s - 1) + v // 4 + 1)
                act.activation(prob[:, v, :], tp[v % 2][:], ACT.Exp, scale=SM_SCALE).then_inc(s_exp, 1)

            def att_hi(s, hg):
                act.wait_ge(s_att, s + 1)
                act.copy(attT_hi[:, hg, :], att[:]).then_inc(s_att_hi, 1)

            def ln_apply(b):
                act.wait_ge(s_nm, b)
                for t in range(TT):
                    act.activation(xh[:, t, :], xh[:, t, :], ACT.Identity, bias=ln_nm[:, t:t + 1],
                                   scale=ln_rs[:, t:t + 1]).then_inc(s_h, 1)

            def ffn_ln_apply(p, t, tail=False):
                act.wait_ge(s_fnm, p + 1)
                dst, _ = quant_bufs(t, tail)
                if tail and t == 2:
                    act.wait_ge(s_pv, 3 * G * B)
                act.activation(dst, x1[:, t, :], ACT.Identity, bias=f_nm[:, t:t + 1],
                               scale=f_rs[:, t:t + 1]).then_inc(s_h2, 1)

            def wffn_split_hi(t):
                act.wait_ge(s_wq_T, t + 1)
                act.copy(wffn_hi[:, :, t * P:(t + 1) * P],
                         slot[t][:].rearrange("p (g n) -> p g n", g=G)).then_inc(s_wffn_hi, 1)

            def q8_copy(p, t):
                n = TT * p + t
                act.wait_ge(s_qT, 2 + n + 1)
                act.copy(q8T[:].rearrange("p g n -> p (g n)"), slot[t % 2][:].bitcast(BF16)[:, 0:D]).then_inc(s_qTc, 1)

            def slot_work(b, hg, k, first, last):
                if hg == 1 and not last:
                    for t in H_AT[k]:
                        h_hi(b + 1, t)
                if first and hg == 0 and k in (2, 3):
                    wffn_split_hi(k)
                if hg >= 2 and not first and k in Q8_AT:
                    q8_copy(b - 1, 2 * (hg - 2) + Q8_AT.index(k))

            def body(b, first, last):
                for hg in range(G):
                    s = 4 * b + hg
                    more2 = not (last and hg >= 2)
                    if hg == 0 and not last:
                        act.wait_ge(s_hT, TT * (b + 1))
                        act.dma_start(xh[:], x_t[bass.ds(b + 1, 1)].rearrange("o p t d -> p (o t) d")).then_inc(s_x, 16)
                    if hg >= 2 and not first:
                        ffn_ln_apply(b - 1, 2 * (hg - 2))
                    if more2:
                        copy_qkv(s + 2, (hg + 2) % G, 0)
                    if not (last and hg == 3):
                        qk_hi(s + 1)
                    if hg >= 2 and not first:
                        ffn_ln_apply(b - 1, 2 * (hg - 2) + 1)
                    if more2:
                        for t in range(1, TT - 1):
                            copy_qkv(s + 2, (hg + 2) % G, t)
                    act.wait_ge(s_mT, s + 1)
                    if not (first and hg == 0):
                        act.wait_ge(s_m, 16 * s)
                    act.mul(negmax[:], sp_[0][0:HG * TT, 0:P], -1.0).then_inc(s_mneg, 1)
                    act.wait_ge(s_mneg, s + 1)
                    act.dma_start(f(q_stack[SHIFT_ROW:SHIFT_ROW + 1, hg % 2, :, :]), f(negmax[:])).then_inc(s_m, 16)
                    if more2:
                        copy_qkv(s + 2, (hg + 2) % G, TT - 1)
                        square(s + 2)
                    for k in range(5):
                        slot_work(b, hg, k, first, last)
                        exp(s, 2 * k)
                        exp(s, 2 * k + 1)
                        if k == 1 and hg == 0 and not first:
                            att_hi(s - 1, (hg - 1) % G)
                    if hg == 0 and not last:
                        ln_apply(b + 1)
                    if first and hg == 1:
                        act.wait_ge(s_wout_ld, 16)
                        act.copy(wout_hi[:], x1[:]).then_inc(s_wout_hi, 1)
                    if hg > 0:
                        if hg == 1 and not first:
                            act.wait_ge(s_op, TT * b)
                        att_hi(s - 1, (hg - 1) % G)

            def split_hi(lo, hi, i):
                act.copy(of_groups(wqkv_hi[:, i, :], lo, hi), of_groups(wq_stage[i], lo, hi)).then_inc(s_whi, 1)

            for i in range(G):
                act.wait_ge(s_wload[i], 16)
                split_hi(*W_PARTS[0], i)
            for i in range(G):
                h_hi(0, i)
            act.wait_ge(s_wrest, 16 * G)
            for part in (1, 2):
                for i in range(G):
                    split_hi(*W_PARTS[part], i)
            for t in range(TT):
                copy_qkv(0, 0, t)
            square(0)
            for t in range(TT):
                copy_qkv(1, 1, t)
            qk_hi(0)
            square(1)
            for t in range(2):
                wffn_split_hi(t)
            act.wait_ge(s_wlo, G * len(W_PARTS))
            batches(act, body)
            att_hi(G * B - 1, 3)
            for t in range(TT):
                ffn_ln_apply(B - 1, t, True)
            for t in range(TT):
                q8_copy(B - 1, t)

        @block.vector
        def _(dve):
            def ln_stats(b):
                dve.wait_ge(s_x, 16 * (b + 1))
                for t in range(TT):
                    dve.bn_stats(ln_st[:, t, :], xh[:, t, :]).then_inc(s_st, 1)
                dve.wait_ge(s_st, TT * (b + 1))
                dve.tensor_copy(wait_v[:], ones[:, 0:1])
                for t in range(TT):
                    dve.bn_aggr(ln_mv[:, t, :], ln_st[:, t, :]).then_inc(s_mv, 1)
                dve.wait_ge(s_mv, TT * (b + 1))
                dve.tensor_scalar(ln_var[:], ln_mv[:, :, 1], LN_EPS, None, ALU.add).then_inc(s_var, 1)

            def ln_shift(b):
                dve.wait_ge(s_rs, b + 1)
                dve.scalar_tensor_tensor(out=ln_nm[:], in0=ln_mv[:, :, 0], scalar=-1.0, in1=ln_rs[:],
                                         op0=ALU.mult, op1=ALU.mult).then_inc(s_nm, 1)

            def h_lo(b, tiles):
                for t in tiles:
                    dve.wait_ge(s_hT_hi, TT * b + t + 1)
                    dve.tensor_tensor(hT_lo[:, t, :, :].rearrange("p g n -> p (g n)"), slot[t][:],
                                      f(hT_hi[:, t, :, :]).rearrange("p g n -> p (g n)"),
                                      ALU.subtract).then_inc(s_hT_lo, 1)

            def square_sums(s):
                dve.wait_ge(s_sq, s + 1)
                dve.tensor_reduce(ss[:], tmp[:].rearrange("p t (h n) -> p (t h) n", n=HD), AX.X, ALU.add).then_inc(s_ss, 1)
                dve.wait_ge(s_ss, s + 1)
                dve.tensor_scalar(ssv[:], ss[:], 1.0 / HD, RMS_EPS, ALU.mult, ALU.add).then_inc(s_ssv, 1)

            def rotated(s):
                dve.wait_ge(s_sin, 4 * (s + 1))
                dve.wait_ge(s_cos, 2 * (s + 1))
                dve.tensor_tensor(rot[:], rot[:], tmp[:], ALU.add).then_inc(s_rsum, 1)

            def qk_lo(s):
                for i in range(2):
                    dve.wait_ge(s_qk_hi, 2 * s + i + 1)
                    if i == 0 and not (isinstance(s, int) and s == 0):
                        dve.wait_ge(s_bounce[1], 16 * s)
                    dve.tensor_tensor(qkT_lo[:, i, :], tp[i][:], f(qkT_hi[:, i, :]), ALU.subtract).then_inc(s_qk_lo, 1)

            def row_max(s, hg, u):
                if u == 0 and not (isinstance(s, int) and s < 2):
                    dve.wait_ge(s_mT, s - 1)
                m = rowmax[:, hg % 2, :].rearrange("p (j t) -> p j t", t=TT)
                t, heads = S_UNITS[u]
                dve.wait_ge(s_S, NS * s + u + 1)
                w = (t + 1) * P
                src = sp_[(NS * hg + u) % 2][:, 0:w * len(heads)].rearrange("p (j n) -> p j n", n=w)
                dve.tensor_reduce(m[:, heads[0]:heads[-1] + 1, t], src, AX.X, ALU.max).then_inc(s_max, 1)

            def normalise(s, k):
                if k == 0:
                    dve.wait_ge(s_pv, 3 * (s + 1))
                    if not (isinstance(s, int) and s == 0):
                        dve.wait_ge(s_att_lo, s)
                    dve.transpose(att[:], dn[:]).then_inc(s_dt, 1)
                elif k == 1:
                    dve.wait_ge(s_dt, s + 1)
                    dve.reciprocal(den_r[:], att[:].rearrange("p (c n) -> p c n", n=HD)[:, :, 0]).then_inc(s_dr, 1)
                elif k == 2:
                    dve.wait_ge(s_dr, s + 1)
                    dve.transpose(att[:], den_r[:].unsqueeze(2).to_broadcast([P, N // HD, HD])).then_inc(s_db, 1)
                else:
                    dve.wait_ge(s_db, s + 1)
                    dve.tensor_tensor(att[:], pv[:], att[:], ALU.mult).then_inc(s_att, 1)

            def quantise(k, src, scale, done, at, y=y[:], mag=mag[:]):
                blk = src.rearrange("p (g n) -> p g n", g=G)
                if k > 0:
                    dve.wait_ge(done, at + k)
                if k == 0:
                    i = dve.tensor_reduce(amax[:], blk, AX.X, ALU.max, apply_absolute_value=True)
                elif k == 1:
                    i = dve.tensor_scalar(scale, amax[:], 1.0 / FP8_MAX, None, ALU.mult)
                elif k == 2:
                    i = dve.reciprocal(rscl[:], scale)
                elif k == 3:
                    i = dve.tensor_tensor(y.rearrange("p (g n) -> p g n", g=G), blk,
                                          rscl[:].unsqueeze(2).to_broadcast([P, G, P]), ALU.mult)
                elif k == 4:
                    i = dve.tensor_scalar(mag.bitcast(I32), y.bitcast(I32), EXPONENT_BITS, None, ALU.bitwise_and)
                else:
                    i = dve.tensor_scalar(mag, mag, FP8_MIN_NORMAL, ROUND_4BIT, ALU.max, ALU.mult)
                i.then_inc(done, 1)

            def ffn_moments(p):
                dve.wait_ge(s_fst, 9 * p + TT)
                dve.tensor_copy(wait_v[:], ones[:, 0:1])
                for t in range(TT):
                    dve.bn_aggr(f_mv[:, t, :], f_st[:, t, :]).then_inc(s_fst, 1)
                dve.wait_ge(s_fst, 9 * p + 2 * TT)
                dve.tensor_scalar(f_var[:], f_mv[:, :, 1], LN_EPS, None, ALU.add).then_inc(s_fst, 1)

            def ffn_shift(p):
                dve.wait_ge(s_frs, p + 1)
                dve.scalar_tensor_tensor(out=f_nm[:], in0=f_mv[:, :, 0], scalar=-1.0, in1=f_rs[:],
                                         op0=ALU.mult, op1=ALU.mult).then_inc(s_fnm, 1)

            def ffn_quant(p, t, k, tail=False):
                if k == 0:
                    dve.wait_ge(s_h2, TT * p + t + 1)
                val, step = quant_bufs(t, tail)
                quantise(k, val, scl[:, t, :], s_q[t], QC * p, val, step)

            def ffn_sum(p, t):
                n = TT * p + t
                for g in range(G):
                    dve.wait_ge(s_ff, G * n + g + 1)
                    if g:
                        dve.wait_ge(s_acc, summed(G * n + g))
                    a = x1[:, t, :]
                    dve.scalar_tensor_tensor(out=a, in0=slot[ffn_bank(t, g)][:], scalar=scl[:, t, g:g + 1],
                                             in1=a, op0=ALU.mult, op1=ALU.add).then_inc(s_acc, 1)

            def out_sum(p, t):
                if t == 0:
                    dve.wait_ge(s_x1l, 16 * (p + 1))
                dve.wait_ge(s_op, TT * p + t + 1)
                dve.tensor_tensor(x1[:, t, :], slot[t][:], x1[:, t, :], ALU.add).then_inc(s_x1, 1)

            def ffn_stats(p, t):
                dve.wait_ge(s_x1, TT * p + t + 1)
                dve.bn_stats(f_st[:, t, :], x1[:, t, :]).then_inc(s_fst, 1)

            def wffn_quant(t):
                if t == 0:
                    dve.wait_ge(s_wffn_ld, 16 * TT)
                at = (QC + 1) * t
                for k in range(QC_V):
                    quantise(k, wffn_stage[t], scl[:, 0, :], s_wq, at)
                dve.wait_ge(s_wq, at + QC_V)
                dve.tensor_tensor(y[:], y[:], mag[:], ALU.add).then_inc(s_wq, 1)
                dve.wait_ge(s_wq, at + QC_V + 1)
                dve.tensor_tensor(y[:], y[:], mag[:], ALU.subtract).then_inc(s_wq, 1)
                dve.wait_ge(s_wq, at + QC)
                dve.tensor_tensor(wffn_stage[t].rearrange("p (g n) -> p g n", g=G), y[:].rearrange("p (g n) -> p g n", g=G),
                                  scl[:, 0, :].unsqueeze(2).to_broadcast([P, G, P]), ALU.mult).then_inc(s_wq, 1)
                dve.wait_ge(s_wq, at + QC + 1)

            def wffn_split(t):
                dve.wait_ge(s_wffn_hi, t + 1)
                cols = slice(t * P, (t + 1) * P)
                dve.tensor_tensor(wffn_lo[:, :, cols], slot[t][:].rearrange("p (g n) -> p g n", g=G),
                                  f(wffn_hi[:, :, cols]), ALU.subtract).then_inc(s_wffn_lo, 1)

            def body(b, first, last):
                for hg in range(G):
                    s = 4 * b + hg
                    more2 = not (last and hg >= 2)
                    quant = [2 * (hg - 2), 2 * (hg - 2) + 1] if hg >= 2 and not first else []
                    for u in range(NS):
                        row_max(s, hg, u)
                        if u == 5 and not (last and hg == 3):
                            qk_lo(s + 1)
                        if hg == 2 and u == 0 and not first:
                            ffn_shift(b - 1)
                        if quant and 1 <= u <= QC_V:
                            ffn_quant(b - 1, quant[0], u - 1)
                        if quant and u > QC_V:
                            ffn_quant(b - 1, quant[1], u - QC_V - 1)
                    if hg == 0 and not last:
                        ln_stats(b + 1)
                    if quant:
                        for k in range(NS - 1 - QC_V, QC_V):
                            ffn_quant(b - 1, quant[1], k)
                    for k in range(4):
                        if k == 0 and more2:
                            square_sums(s + 2)
                        if not (first and hg == 0):
                            normalise(s - 1, k)
                    if first and hg == 0:
                        wffn_quant(3)
                        for t in (2, 3):
                            wffn_split(t)
                    if hg == 0 and not last:
                        ln_shift(b + 1)
                    if quant:
                        ffn_sum(b - 1, quant[0])
                    if more2:
                        rotated(s + 2)
                    if hg == 0 and not first:
                        for t in (0, 1):
                            out_sum(b - 1, t)
                            ffn_stats(b - 1, t)
                    if first and hg == 2:
                        dve.wait_ge(s_wout_hi, 1)
                        dve.tensor_tensor(wout_lo[:], x1[:], f(wout_hi[:]), ALU.subtract).then_inc(s_wout_lo, 1)
                    if hg == 1:
                        if not first:
                            for t in (2, 3):
                                out_sum(b - 1, t)
                                ffn_stats(b - 1, t)
                            ffn_moments(b - 1)
                        if not last:
                            h_lo(b + 1, range(TT))
                    if quant:
                        ffn_sum(b - 1, quant[1])

            dve.memset(ones[:], 1.0).then_inc(s_const_v, 1)
            dve.wait_ge(s_const_v, 1)
            dve.memset(wait_v[:], 0.0).then_inc(s_acc, 1)
            for i in range(2):
                dve.memset(q8[:, i, 0:2], 0.0).then_inc(s_qT, 1)
            ln_stats(0)
            dve.wait_ge(s_rs, 1)
            for t in range(TT):
                dve.tensor_scalar(xh[:, t, :], xh[:, t, :], ln_mv[:, t, 0:1], ln_rs[:, t:t + 1],
                                  ALU.subtract, ALU.mult).then_inc(s_h, 1)
            h_lo(0, range(TT))
            def split_lo(part):
                lo, hi = W_PARTS[part]
                for i in range(G):
                    dve.wait_ge(s_whi, G * part + i + 1)
                    dve.tensor_tensor(of_groups(wqkv_lo[:, i, :], lo, hi), of_groups(wq_stage[i], lo, hi),
                                      f(of_groups(wqkv_hi[:, i, :], lo, hi)), ALU.subtract).then_inc(s_wlo, 1)

            split_lo(0)
            split_lo(1)
            dve.wait_ge(s_tload, 48)
            for i in range(2):
                dve.tensor_tensor(rope_c[:, i], table[:, 0], gamma[:, i, :].unsqueeze(1).to_broadcast([P, TT, HD]),
                                  ALU.mult).then_inc(s_fold, 1)
                for h in range(2):
                    dve.tensor_tensor(rope_s[:, i, :, h * HALF:(h + 1) * HALF], table[:, 1, :, h * HALF:(h + 1) * HALF],
                                      gamma[:, i, (1 - h) * HALF:(2 - h) * HALF].unsqueeze(1).to_broadcast([P, TT, HALF]),
                                      ALU.mult).then_inc(s_fold, 1)
            dve.wait_ge(s_fold, 6)
            split_lo(2)
            wffn_quant(0)
            square_sums(0)
            sin_part(dve, 0)
            rotated(0)
            wffn_quant(1)
            qk_lo(0)
            square_sums(1)
            sin_part(dve, 1)
            rotated(1)
            for t in range(2):
                wffn_split(t)
            wffn_quant(2)
            batches(dve, body)
            for k in range(4):
                normalise(G * B - 1, k)
            p = B - 1
            for t in range(TT):
                out_sum(p, t)
                ffn_stats(p, t)
            ffn_moments(p)
            ffn_shift(p)
            for t in range(TT):
                for k in range(QC_V):
                    ffn_quant(p, t, k, True)
            for t in range(TT):
                ffn_sum(p, t)

        @block.gpsimd
        def _(pool):
            def power(dst, src, done):
                pool.tensor_tensor(dst, src, half_neg[:, 0:src.shape[-1]], ALU.pow).then_inc(done, 1)

            def cos_part(s):
                raw = qk[:].rearrange("p t (i j n) -> p t i j n", i=2, j=HG)
                r = rot[:].rearrange("p t (i j n) -> p t i j n", i=2, j=HG)
                pool.wait_ge(s_qk, TT * (s + 1))
                if not (isinstance(s, int) and s == 0):
                    pool.wait_ge(s_qkT, 2 * s)
                for i in range(2):
                    cos = rope_c[:, i, :, :].unsqueeze(2).to_broadcast([P, TT, HG, HD])
                    pool.tensor_tensor(r[:, :, i], raw[:, :, i], cos, ALU.mult).then_inc(s_cos, 1)

            def head_norm(s):
                pool.wait_ge(s_ssv, s + 1)
                if not (isinstance(s, int) and s == 0):
                    pool.wait_ge(s_rope, s)
                power(rs[:], ssv[:], s_rrs)
                pool.wait_ge(s_rsum, s + 1)
                pool.wait_ge(s_rrs, s + 1)
                r = rot[:].rearrange("p t (h n) -> p (t h) n", n=HD)
                pool.tensor_tensor(r, r, rs[:].unsqueeze(2).to_broadcast([P, 2 * HG * TT, HD]), ALU.mult).then_inc(s_rope, 1)

            def round_fp8(p, t, tail=False):
                val, step = quant_bufs(t, tail)
                q, at = s_q[t], QC * p + QC_V
                pool.wait_ge(q, at)
                pool.tensor_tensor(val, val, step, ALU.add).then_inc(q, 1)
                pool.wait_ge(q, at + 1)
                pool.wait_ge(s_qT, TT * p + t + 1)
                pool.tensor_tensor(q8[:, t % 2, :], val, step, ALU.subtract).then_inc(q, 1)

            def att_lo(s, hg):
                pool.wait_ge(s_att_hi, s + 1)
                pool.tensor_tensor(attT_lo[:, hg, :], att[:], f(attT_hi[:, hg, :]), ALU.subtract).then_inc(s_att_lo, 1)

            def ln_power(b):
                pool.wait_ge(s_var, b + 1)
                power(ln_rs[:], ln_var[:], s_rs)

            def ffn_power(p):
                pool.wait_ge(s_fst, 9 * (p + 1))
                power(f_rs[:], f_var[:], s_frs)

            def body(b, first, last):
                for hg in range(G):
                    s = 4 * b + hg
                    if hg == 0 and not last:
                        ln_power(b + 1)
                    if hg == 2 and not first:
                        ffn_power(b - 1)
                    t = 2 * (hg - 2)
                    if hg >= 2 and not first:
                        round_fp8(b - 1, t)
                        round_fp8(b - 1, t + 1)
                    if not (last and hg >= 2):
                        cos_part(s + 2)
                    if hg == 0 and not first:
                        att_lo(s - 1, (hg - 1) % G)
                    if not (last and hg >= 2):
                        sin_part(pool, s + 2)
                    if not (last and hg >= 2):
                        head_norm(s + 2)
                    if hg > 0:
                        att_lo(s - 1, (hg - 1) % G)

            def step(ins, count=[0]):
                count[0] += 1
                ins.then_inc(s_pool_c, 1)
                pool.wait_ge(s_pool_c, count[0])

            step(pool.memset(half_neg[:], -0.5))
            step(pool.memset(ident[:], 0.0))
            pool.affine_select(ident[:], ident[:], pattern=[[-1, P]], compare_op=ALU.not_equal, fill=1.0,
                               base=0, channel_multiplier=1).then_inc(s_ident, 1)
            ln_power(0)
            pool.wait_ge(s_ident, 1)
            step(pool.tensor_copy(ident_bf[:], ident[:]))
            step(pool.memset(mask_q[:], 0.0))
            step(pool.affine_select(mask_q[:], mask_q[:], pattern=[[-1, P]], compare_op=ALU.is_ge, fill=NEG,
                                    base=0, channel_multiplier=1))
            step(pool.memset(mask_k[:], 0.0))
            step(pool.memset(f(k_stack[SHIFT_ROW:SHIFT_ROW + HD, :, :, :]), 1.0))
            pool.affine_select(mask_k[:], mask_k[:], pattern=[[1, P]], compare_op=ALU.is_ge, fill=NEG,
                               base=0, channel_multiplier=-1).then_inc(s_const, 1)
            pool.wait_ge(s_fold, 6)
            for g in range(2):
                cos_part(g)
                head_norm(g)
            batches(pool, body)
            att_lo(G * B - 1, 3)
            ffn_power(B - 1)
            for t in range(TT):
                round_fp8(B - 1, t, True)


_NAMES = ["L0_attn_x", "L0_attn_w_qkv", "L0_attn_w_out", "L0_attn_q_gamma", "L0_attn_k_gamma", "L0_ffn_weight"]


def kernel(**inputs):
    import numpy as _np
    import concourse.bacc as _bacc
    from concourse import mybir as _mybir
    from concourse.bass_utils import run_bass_kernel_spmd as _run

    nc = _bacc.Bacc("TRN2", target_bir_lowering=False, num_devices=1, dynamic_dma_scratch_size=512)
    arrays = {f"in_{n}": _np.ascontiguousarray(inputs[n]) for n in _NAMES}
    arrays["in_rope"] = rope_tables()
    args = [nc.dram_tensor(n, a.shape, _mybir.dt.from_np(a.dtype), kind="ExternalInput").ap() for n, a in arrays.items()]
    args.append(nc.dram_tensor("out_0", (B, N, D), _mybir.dt.float32, kind="ExternalOutput").ap())
    build_program(nc, *args)
    r = _run(nc, [arrays], core_ids=[0])
    return r.results[0]["out_0"]
```
